# Optimizing a Trainium2 kernel written in Bass

```python
import numpy as np
import jax
import jax.numpy as jnp

def _softmax(x, axis=-1):
    return jax.nn.softmax(x, axis=axis)

def _gelu(x):
    return jax.nn.gelu(x, approximate=True)

def _silu(x):
    return jax.nn.silu(x)

def _sigmoid(x):
    return jax.nn.sigmoid(x)

def _layernorm(x, axis=-1, eps=1e-05):
    m = jnp.mean(x, axis=axis, keepdims=True)
    v = jnp.var(x, axis=axis, keepdims=True)
    return (x - m) / jnp.sqrt(v + eps)

def _scatter_add(tgt, idx, src, axis=0):
    return tgt.at[idx].add(src)

def _segment_sum(src, seg, n):
    return jax.ops.segment_sum(src, seg, n)
kernel_name = 'mk_conv_seq_d2_conv_nchw512_r2_a267be'

def setup_inputs(seed: int=0):
    np.random.seed(seed)
    _w = jnp.asarray

    def _rec_inputs():
        import jax
        import jax.numpy as jnp
        _gk = jax.random.key(seed)
        x = -0.0002928 + 1 * jax.random.normal(jax.random.fold_in(_gk, 1), (8, 256, 32, 32), jnp.float32)
        return x
    x = _rec_inputs()

    def _L0_conv_setup():
        import jax, jax.numpy as jnp
        import numpy as np
        B, C, H, W = (8, 256, 32, 32)
        NUM_HEADS = 8
        GROUPS = 32
        EPS = 1e-05

        def _group_norm(x, gamma, beta):
            b, c, h, w = x.shape
            xg = x.reshape(b, GROUPS, c // GROUPS, h, w)
            mean = xg.mean(axis=(2, 3, 4), keepdims=True)
            var = xg.var(axis=(2, 3, 4), keepdims=True)
            xn = ((xg - mean) * jax.lax.rsqrt(var + EPS)).reshape(b, c, h, w)
            return xn * gamma[None, :, None, None] + beta[None, :, None, None]
        key = jax.random.key(seed)
        ks = jax.random.split(key, 6)
        x = jax.random.normal(ks[0], (B, C, H, W), dtype=jnp.float32)
        gamma = jnp.ones((C,), dtype=jnp.float32)
        beta = jnp.zeros((C,), dtype=jnp.float32)
        w_qkv = jax.random.normal(ks[1], (3 * C, C), dtype=jnp.float32) * (1.0 / np.sqrt(C))
        b_qkv = jax.random.normal(ks[2], (3 * C,), dtype=jnp.float32) * 0.01
        w_proj = jax.random.normal(ks[3], (C, C), dtype=jnp.float32) * (0.02 / np.sqrt(C))
        b_proj = jax.random.normal(ks[4], (C,), dtype=jnp.float32) * 0.01
        return {'x': x, 'gamma': gamma, 'beta': beta, 'w_qkv': w_qkv, 'b_qkv': b_qkv, 'w_proj': w_proj, 'b_proj': b_proj}
    _L0_conv_all = _L0_conv_setup()
    _L0_conv_in = {k: v for k, v in _L0_conv_all.items() if k in ('gamma', 'beta', 'w_qkv', 'b_qkv', 'w_proj', 'b_proj')}
    del _L0_conv_all

    def _L1_conv_setup():
        import jax, jax.numpy as jnp
        import numpy as np
        GROUPS = 32
        EPS = 1e-05

        def group_norm(x, w, b):
            B, C, H, W = x.shape
            xg = x.reshape(B, GROUPS, C // GROUPS, H, W)
            mu = xg.mean(axis=(2, 3, 4), keepdims=True)
            var = xg.var(axis=(2, 3, 4), keepdims=True)
            xn = ((xg - mu) / jnp.sqrt(var + EPS)).reshape(B, C, H, W)
            return xn * w[None, :, None, None] + b[None, :, None, None]
        key = jax.random.key(seed)
        ks = jax.random.split(key, 4)
        B, C, H, W = (8, 256, 32, 32)
        x = jax.random.normal(ks[0], (B, C, H, W), dtype=jnp.float32)
        gn_w = jnp.ones((C,), dtype=jnp.float32)
        gn_b = jnp.zeros((C,), dtype=jnp.float32)
        qkv_w = jax.random.normal(ks[1], (3 * C, C), dtype=jnp.float32) * (1.0 / np.sqrt(C))
        proj_w = jax.random.normal(ks[2], (C, C), dtype=jnp.float32) * (1.0 / np.sqrt(C))
        proj_b = jnp.zeros((C,), dtype=jnp.float32)
        return {'x': x, 'gn_w': gn_w, 'gn_b': gn_b, 'qkv_w': qkv_w, 'proj_w': proj_w, 'proj_b': proj_b, 'num_heads': 8}
    _L1_conv_all = _L1_conv_setup()
    _L1_conv_in = {k: v for k, v in _L1_conv_all.items() if k in ('gn_w', 'gn_b', 'qkv_w', 'proj_w', 'proj_b')}
    del _L1_conv_all
    return {'x': x, 'L0_conv_gamma': _L0_conv_in['gamma'], 'L0_conv_beta': _L0_conv_in['beta'], 'L0_conv_w_qkv': _L0_conv_in['w_qkv'], 'L0_conv_b_qkv': _L0_conv_in['b_qkv'], 'L0_conv_w_proj': _L0_conv_in['w_proj'], 'L0_conv_b_proj': _L0_conv_in['b_proj'], 'L1_conv_gn_w': _L1_conv_in['gn_w'], 'L1_conv_gn_b': _L1_conv_in['gn_b'], 'L1_conv_qkv_w': _L1_conv_in['qkv_w'], 'L1_conv_proj_w': _L1_conv_in['proj_w'], 'L1_conv_proj_b': _L1_conv_in['proj_b']}

def reference(x, L0_conv_gamma, L0_conv_beta, L0_conv_w_qkv, L0_conv_b_qkv, L0_conv_w_proj, L0_conv_b_proj, L1_conv_gn_w, L1_conv_gn_b, L1_conv_qkv_w, L1_conv_proj_w, L1_conv_proj_b):
    import jax
    import jax.numpy as jnp

    def _L0_conv_ref(x, gamma, beta, w_qkv, b_qkv, w_proj, b_proj):
        import jax, jax.numpy as jnp
        import numpy as np
        B, C, H, W = (8, 256, 32, 32)
        NUM_HEADS = 8
        GROUPS = 32
        EPS = 1e-05

        def _group_norm(x, gamma, beta):
            b, c, h, w = x.shape
            xg = x.reshape(b, GROUPS, c // GROUPS, h, w)
            mean = xg.mean(axis=(2, 3, 4), keepdims=True)
            var = xg.var(axis=(2, 3, 4), keepdims=True)
            xn = ((xg - mean) * jax.lax.rsqrt(var + EPS)).reshape(b, c, h, w)
            return xn * gamma[None, :, None, None] + beta[None, :, None, None]
        b, c, h, w = x.shape
        nh = NUM_HEADS
        hd = c // nh
        s = h * w
        scale = 1.0 / float(hd) ** 0.25
        xn = _group_norm(x, gamma, beta)
        qkv = jnp.einsum('bchw,oc->bohw', xn, w_qkv) + b_qkv[None, :, None, None]
        qkv = qkv.reshape(b, nh, 3 * hd, s)
        q, k, v = (qkv[:, :, :hd], qkv[:, :, hd:2 * hd], qkv[:, :, 2 * hd:])
        m = jnp.einsum('bhcs,bhct->bhst', q * scale, k * scale)
        m = jax.nn.softmax(m, axis=-1)
        a = jnp.einsum('bhst,bhct->bhcs', m, v)
        a = a.reshape(b, c, h, w)
        out = jnp.einsum('bchw,oc->bohw', a, w_proj) + b_proj[None, :, None, None]
        return x + out

    def _L1_conv_ref(x, gn_w, gn_b, qkv_w, proj_w, proj_b, num_heads):
        import jax, jax.numpy as jnp
        import numpy as np
        GROUPS = 32
        EPS = 1e-05

        def group_norm(x, w, b):
            B, C, H, W = x.shape
            xg = x.reshape(B, GROUPS, C // GROUPS, H, W)
            mu = xg.mean(axis=(2, 3, 4), keepdims=True)
            var = xg.var(axis=(2, 3, 4), keepdims=True)
            xn = ((xg - mu) / jnp.sqrt(var + EPS)).reshape(B, C, H, W)
            return xn * w[None, :, None, None] + b[None, :, None, None]
        B, C, H, W = x.shape
        N = H * W
        head_dim = C // num_heads
        xn = group_norm(x, gn_w, gn_b)
        qkv = jnp.einsum('oc,bcn->bon', qkv_w, xn.reshape(B, C, N))
        qkv = qkv.reshape(B * num_heads, 3 * head_dim, N)
        q, k, v = jnp.split(qkv, 3, axis=1)
        scale = 1.0 / np.sqrt(np.sqrt(head_dim))
        attn = jax.nn.softmax(jnp.einsum('bct,bcs->bts', q * scale, k * scale), axis=-1)
        h = jnp.einsum('bts,bcs->bct', attn, v)
        h = h.reshape(B, C, N)
        out = jnp.einsum('oc,bcn->bon', proj_w, h) + proj_b[None, :, None]
        return out.reshape(B, C, H, W) + x

    def _gn(v, G=32, eps=1e-05):
        B_, C_, H_, W_ = v.shape
        g = v.reshape(B_, G, C_ // G, H_, W_)
        m = jnp.mean(g, axis=(2, 3, 4), keepdims=True)
        s = jnp.var(g, axis=(2, 3, 4), keepdims=True)
        return ((g - m) / jnp.sqrt(s + eps)).reshape(v.shape)

    def _ln_c(v, eps=1e-06):
        m = jnp.mean(v, axis=1, keepdims=True)
        s = jnp.var(v, axis=1, keepdims=True)
        return (v - m) / jnp.sqrt(s + eps)

    def _ln_t(v, eps=1e-05):
        m = jnp.mean(v, axis=-1, keepdims=True)
        s = jnp.var(v, axis=-1, keepdims=True)
        return (v - m) / jnp.sqrt(s + eps)

    def _to_tokens(v):
        B_, C_, H_, W_ = v.shape
        return v.reshape(B_, C_, H_ * W_).transpose(0, 2, 1)

    def _from_tokens(t, like):
        B_, C_, H_, W_ = like.shape
        return t.transpose(0, 2, 1).reshape(B_, C_, H_, W_)
    x = _L0_conv_ref(x, L0_conv_gamma, L0_conv_beta, L0_conv_w_qkv, L0_conv_b_qkv, L0_conv_w_proj, L0_conv_b_proj)
    x = _L1_conv_ref(x, L1_conv_gn_w, L1_conv_gn_b, L1_conv_qkv_w, L1_conv_proj_w, L1_conv_proj_b, 8)
    return x

_drawn_inputs = setup_inputs


def setup_inputs(seed=0):
    import zlib

    import numpy as np

    out = dict(_drawn_inputs(seed))
    spreads = {'L0_conv_gamma': (1.0, 0.6),
     'L0_conv_beta': (0.0, 0.8),
     'L1_conv_gn_w': (1.0, 0.2),
     'L1_conv_gn_b': (0.0, 0.1),
     'L1_conv_proj_b': (0.0, 0.1)}
    factors = {'L0_conv_w_qkv': 8.0,
     'L0_conv_b_qkv': 8.0,
     'L0_conv_w_proj': 8.0,
     'L0_conv_b_proj': 13.403}
    for name, (base, spread) in spreads.items():
        noise = np.random.default_rng([zlib.crc32(name.encode()), seed]).standard_normal(out[name].shape)
        drawn = base * np.exp(spread * noise) if base else spread * noise
        out[name] = jnp.asarray(drawn.astype(out[name].dtype))
    for name, factor in factors.items():
        out[name] = (out[name] * factor).astype(out[name].dtype)
    return out
```

```python
from contextlib import ExitStack

import numpy as np

import concourse.bass as bass
from concourse import mybir

F32 = mybir.dt.float32
F32R = mybir.dt.float32r
ALU = mybir.AluOpType
ACT = mybir.ActivationFunctionType
AX = mybir.AxisListType

LAYERS, B, C, S = 2, 8, 256, 1024
HEADS, GROUPS = 8, 32
EPS = 1e-5
HD = C // HEADS
SCALE = float(HD) ** -0.5
P = 128
CT = C // P
HG = HEADS // CT
NT = S // P
HALF = 512
NH = S // HALF
BLOCKS = LAYERS * B
SLOTS = BLOCKS * CT
UNITS = NH * NT * HG
KROWS = 3 * HD
MROW = KROWS
POOLED = 6
ADDS = POOLED - 1
QUARTERS = 2 * NH
STAGE_DMAS = 2 * 3 * HG
PV_LAG = 2
SUMS_AT = 5
MAX_FROM, MAX_TO = 14, 60
PROJ_AT = (10, 13, 16, 19)
V_AT = (4, 8, 12, 16)
QK_AT = (34, 41, 48, 55)
GN_AT = 20
LOOP_FROM, LOOP_SLOTS = 1, 4
LOOPS = (SLOTS - 4) // LOOP_SLOTS


class Slot:

    def __init__(self, n, j, phase):
        self.n, self.j = n, j
        self.g = phase % 2
        self.qk = phase % 2
        self.v = (phase // 2) % 2
        self.phase = phase


def plain(n):
    return Slot(n, n // 2, n % 4)


def looped(i, k):
    return Slot(LOOP_SLOTS * i + LOOP_FROM + k, 2 * i + (LOOP_FROM + k) // 2, (LOOP_FROM + k) % 4)


def run_slots(eng, slot):
    slot(plain(0), first=True)
    with eng.Fori(0, LOOPS) as i:
        for k in range(LOOP_SLOTS):
            slot(looped(i, k))
    for n in range(LOOP_FROM + LOOPS * LOOP_SLOTS, SLOTS):
        slot(plain(n), has_next=n + 1 < SLOTS, has_second=n + 2 < SLOTS)


def max_units_at(u):
    if not MAX_FROM <= u < MAX_TO:
        return range(0)
    span = MAX_TO - MAX_FROM
    return range((u - MAX_FROM) * UNITS // span, (u - MAX_FROM + 1) * UNITS // span)


MAX_ROWS_AT = {}
for _t in range(NT):
    _last = (_t + 1) * HG * NH - 1
    _u = next(u for u in range(UNITS) if _last in max_units_at(u))
    MAX_ROWS_AT[min(_u + 3, UNITS - 1)] = _t


def attention_layers(nc, x, w_qkv, w_proj, pars, bias_v, bias_proj, ident_in, group_in, out):
    nc.disable_value_cache = True
    ctx = ExitStack()
    with ctx:
        def sb(name, shape, dt=F32):
            return ctx.enter_context(nc.sbuf_tensor(name, shape, dt))

        def bank(name):
            return ctx.enter_context(nc.psum_tensor(name, [P, HALF], F32))

        def sem(name):
            return ctx.enter_context(nc.semaphore(name))

        between = nc.dram_tensor("between", [B, CT, P, S], F32).ap()

        wq = sb("wq", [P, CT, 3 * C])
        wp = sb("wp", [P, CT, C])
        bv = sb("bv", [P, HALF])
        par = sb("par", [P, 2, 8])
        bp = sb("bp", [P, CT])
        ident = sb("ident", [P, P])
        group = sb("group", [P, P])
        ones = sb("ones", [P, HD])
        eps = sb("eps", [P, CT])
        neg_half = sb("neg_half", [P, CT])
        xn = sb("xn", [P, CT, S])
        stats = sb("stats", [P, CT, NH, 6])
        mv = sb("mv", [P, CT, QUARTERS, 2])
        sq4 = sb("sq4", [P, CT, QUARTERS])
        inv_count = sb("inv_count", [P, CT, QUARTERS])
        sq = sb("sq", [P, CT])
        gm = sb("gm", [P, CT, 2])
        var = sb("var", [P, CT])
        rstd = sb("rstd", [P, CT])
        gn_a = sb("gn_a", [P, CT])
        gn_c = sb("gn_c", [P, CT])
        stage = {w: sb("stage_" + w, [P, S], F32R) for w in ("qh", "ql", "kh", "kl")}
        qs = [sb(f"qs{b}", [P, HG, S], F32R) for b in range(2)]
        ks = [sb(f"ks{b}", [P, HG, S], F32R) for b in range(2)]
        v = [sb(f"v{b}", [P, NT, C]) for b in range(2)]
        pt = [sb(f"pt{b}", [P, HG, HALF]) for b in range(4)]
        acc = sb("acc", [P, HG, HALF])
        raw_max = sb("raw_max", [P, 2, HG, NH])
        neg_max = sb("neg_max", [P, 2, HG])
        rden = sb("rden", [P, HALF])
        att = sb("att", [P, CT, S])
        res = sb("res", [P, CT * NH, HALF])

        ps_t = [bank(f"ps_t{b}") for b in range(2)]
        ps_m = [bank(f"ps_m{b}") for b in range(2)]
        ps_v = [bank(f"ps_v{b}") for b in range(2)]
        ps_d = bank("ps_d")
        ps_a = bank("ps_a")

        loaded = sem("constants_loaded")
        weights = sem("weights_loaded")
        wproj_loaded = sem("wproj_loaded")
        x_loaded = sem("x_loaded")
        res_loaded = sem("res_loaded")
        stored = sem("stored")
        staged = sem("staged")
        const_dve = sem("const_dve")
        bn_done = sem("bn_done")
        mv_done = sem("mv_done")
        gm_ready = sem("gm_ready")
        gm_done = sem("gm_done")
        gn_step = sem("gn_step")
        xn_done = sem("xn_done")
        qk_ready = sem("qk_ready")
        qkh_done = sem("qkh_done")
        qkl_done = sem("qkl_done")
        v_ready = sem("v_ready")
        v_done = sem("v_done")
        proj_ready = sem("proj_ready")
        proj_done = sem("proj_done")
        sm_ready = sem("sm_ready")
        max_done = sem("max_done")
        neg_done = sem("neg_done")
        mrow_ready = sem("mrow_ready")
        mrow_done = sem("mrow_done")
        st_ready = sem("st_ready")
        exp_done = sem("exp_done")
        pv_done = sem("pv_done")
        pool_added = sem("pool_added")
        sum_ready = sem("sum_ready")
        rden_done = sem("rden_done")
        norm_done = sem("norm_done")

        block = ctx.enter_context(nc.Block())

        @block.sync
        def _(sp):
            sp.dma_start(ident[:, :], ident_in).then_inc(loaded, 16)
            sp.dma_start(group[:, :], group_in).then_inc(loaded, 16)

            def load_block(layer, src, image, parity):
                for ct in range(CT):
                    sp.dma_start(xn[:, ct, :], src[image, ct]).then_inc(x_loaded, 16)
                sp.dma_start(par[:, parity, :], pars[layer]).then_inc(x_loaded, 16)

            def load_weights(layer):
                sp.dma_start(wq[:, :, :], w_qkv[layer]).then_inc(weights, 16)
                sp.dma_start(bv[:, :], bias_v[layer]).then_inc(weights, 16)

            def load_residual(layer, src, image):
                for ct in range(CT):
                    sp.dma_start(res[:, NH * ct:NH * ct + NH, :],
                                 src[image, ct].rearrange("p (h s) -> p h s", h=NH)).then_inc(res_loaded, 16)
                sp.dma_start(bp[:, :], bias_proj[layer]).then_inc(res_loaded, 16)

            def store_block(dst, j, image):
                for piece in range(CT * NH):
                    sp.wait_ge(proj_done, CT * NH * j + piece + 1)
                    h, ct = piece // CT, piece % CT
                    sp.dma_start(dst[image, ct][:, h * HALF:(h + 1) * HALF],
                                 res[:, NH * ct + h, :]).then_inc(stored, 16)

            def stage_slot(n, b):
                sp.wait_ge(qkl_done, 4 * n + 4)
                for dst, parts in ((ks[b], ("kh", "kl", "kh")), (qs[b], ("qh", "qh", "ql"))):
                    for r, part in enumerate(parts):
                        for h in range(HG):
                            sp.dma_start(dst[HD * r:HD * (r + 1), h, :].bitcast(F32),
                                         stage[part][HD * h:HD * (h + 1), :].bitcast(F32)).then_inc(staged, 16)

            load_weights(0)
            load_block(0, x, 0, 0)
            sp.dma_start(wp[:, :, :], w_proj[0]).then_inc(wproj_loaded, 16)
            stage_slot(0, 0)
            stage_slot(1, 1)
            sp.wait_ge(qk_ready, 8)
            load_block(0, x, 1, 1)

            def body(i, next_layer, done_layer):
                nsrc = x if next_layer == 0 else between
                dsrc, ddst = (x, between) if done_layer == 0 else (between, out)
                for k in range(LOOP_SLOTS):
                    s = looped(i, k)
                    sp.wait_ge(st_ready, UNITS * s.n)
                    stage_slot(s.n + 1, 1 - s.qk)
                    if s.g == 1:
                        continue
                    sp.wait_ge(qk_ready, 4 * (2 * s.j + 2))
                    if isinstance(i, int) and s.j == B - 1:
                        sp.wait_ge(v_done, 4 * B)
                        load_weights(1)
                        sp.wait_ge(weights, 64)
                    load_block(next_layer, nsrc, s.j + 1 - B * next_layer, 1 - s.v)
                    if not (isinstance(s.j, int) and s.j < 2):
                        sp.wait_ge(stored, 16 * CT * NH * (s.j - 1))
                    load_residual(done_layer, dsrc, s.j - 1 - B * done_layer)
                    store_block(ddst, s.j - 1, s.j - 1 - B * done_layer)
                    if isinstance(i, int) and s.j == B:
                        sp.dma_start(wp[:, :, :], w_proj[1]).then_inc(wproj_loaded, 16)
                        sp.wait_ge(wproj_loaded, 32)

            turn = B // 2 - 1
            body(0, 0, 0)
            with sp.Fori(1, turn) as i:
                body(i, 0, 0)
            body(turn, 1, 0)
            with sp.Fori(turn + 1, LOOPS) as i:
                body(i, 1, 1)
            for n in range(LOOP_FROM + LOOPS * LOOP_SLOTS, SLOTS):
                s = plain(n)
                if n + 1 < SLOTS:
                    sp.wait_ge(st_ready, UNITS * n)
                    stage_slot(n + 1, 1 - s.qk)
                if s.g == 0:
                    sp.wait_ge(stored, 16 * CT * NH * (s.j - 1))
                    load_residual(1, between, s.j - 1 - B)
                    store_block(out, s.j - 1, s.j - 1 - B)
            sp.wait_ge(stored, 16 * CT * NH * (BLOCKS - 1))
            load_residual(1, between, B - 1)
            store_block(out, BLOCKS - 1, B - 1)
            sp.wait_ge(stored, 16 * CT * NH * BLOCKS)

        @block.tensor
        def _(pe):
            def aux_free(mrows, sums, stats_done=None):
                if not (isinstance(mrows, int) and mrows == 0):
                    pe.wait_ge(mrow_done, mrows)
                if not (isinstance(sums, int) and sums == 0):
                    pe.wait_ge(rden_done, sums)
                if stats_done is not None:
                    pe.wait_ge(gm_done, stats_done)

            def scores_t(s, u):
                hf, t, h = u // (NT * HG), u // HG % NT, u % HG
                if not (isinstance(s.n, int) and UNITS * s.n + u < 2):
                    pe.wait_ge(exp_done, UNITS * s.n + u - 1)
                if u % (NT * HG) == 0:
                    pe.wait_ge(mrow_done, NT * s.n + (hf + 1) * NT // NH)
                pe.matmul(ps_t[u % 2][:, :], ks[s.qk][0:KROWS + 1, h, t * P:(t + 1) * P],
                          qs[s.qk][0:KROWS + 1, h, hf * HALF:(hf + 1) * HALF],
                          start=True, stop=True).then_inc(st_ready, 1)

            def scores_for_max(n, b, w):
                t, h, kf = w // (HG * NH), w // NH % HG, w % NH
                if w == 0:
                    pe.wait_ge(staged, 16 * STAGE_DMAS * (n + 1))
                if not (isinstance(n, int) and UNITS * n + w < 2):
                    pe.wait_ge(max_done, UNITS * n + w - 1)
                pe.matmul(ps_m[w % 2][:, :], qs[b][0:KROWS, h, t * P:(t + 1) * P],
                          ks[b][0:KROWS, h, kf * HALF:(kf + 1) * HALF],
                          start=True, stop=True).then_inc(sm_ready, 1)

            def max_rows(n, t, sums, stats_done=None):
                pe.wait_ge(neg_done, NT * n + t + 1)
                aux_free(NT * n + t, sums, stats_done)
                for h in range(HG):
                    mm = pe.matmul(ps_a[MROW:MROW + 1, h * P:(h + 1) * P], neg_max[:, t % 2, h:h + 1],
                                   ident[:, :], start=True, stop=True)
                mm.then_inc(mrow_ready, 1)

            def weighted_values(s, hf, t):
                half = NH * s.n + hf
                pe.wait_ge(exp_done, HG * (NT * half + t + 1))
                if t == 0:
                    if not (isinstance(half, int) and half < 2):
                        pe.wait_ge(norm_done, half - 1)
                    if hf == 0:
                        pe.wait_ge(v_done, 4 * s.j + 4)
                for h in range(HG):
                    c = (s.g * HG + h) * HD
                    mm = pe.matmul(ps_v[hf][HD * h:HD * (h + 1), :], v[s.v][:, t, c:c + HD],
                                   pt[t % 4][:, h, :], start=(t == 0), stop=(t == NT - 1))
                mm.then_inc(pv_done, 1)

            def sums(s, hf, mrows):
                half = NH * s.n + hf
                pe.wait_ge(pool_added, ADDS * half + ADDS)
                aux_free(mrows, half)
                tiles = [pt[t % 4] for t in range(POOLED, NT)] + [acc]
                for k, tile in enumerate(tiles):
                    for h in range(HG):
                        mm = pe.matmul(ps_a[HD * h:HD * (h + 1), :], ones[:, :], tile[:, h, :],
                                       start=(k == 0), stop=(k == len(tiles) - 1))
                mm.then_inc(sum_ready, 1)

            def project_qk(n, g, r):
                which, hf = r // NH, r % NH
                c = which * C + g * P
                for kt in range(CT):
                    mm = pe.matmul(ps_d[:, :], wq[:, kt, c:c + P], xn[:, kt, hf * HALF:(hf + 1) * HALF],
                                   start=(kt == 0), stop=(kt == CT - 1))
                mm.then_inc(qk_ready, 1)

            def project_v(r):
                for t in range(2):
                    for kt in range(CT):
                        mm = pe.matmul(ps_d[:, t * C:(t + 1) * C], xn[:, kt, (2 * r + t) * P:(2 * r + t + 1) * P],
                                       wq[:, kt, 2 * C:3 * C], start=(kt == 0), stop=(kt == CT - 1))
                mm.then_inc(v_ready, 1)

            def project_out(piece):
                hf, ct = piece // CT, piece % CT
                for kt in range(CT):
                    mm = pe.matmul(ps_d[:, :], wp[:, kt, ct * P:(ct + 1) * P],
                                   att[:, kt, hf * HALF:(hf + 1) * HALF], start=(kt == 0), stop=(kt == CT - 1))
                mm.then_inc(proj_ready, 1)

            def group_stats(j, mrows, nsums):
                pe.wait_ge(mv_done, MV_STEPS * (j + 1))
                aux_free(mrows, nsums)
                for quarter in range(QUARTERS):
                    mm = pe.matmul(ps_a[:, 0:2 * CT], group[:, :], mv[:, :, quarter, :],
                                   start=(quarter == 0), stop=(quarter == QUARTERS - 1))
                mm.then_inc(gm_ready, 1)

            def slot(s, first=False, has_next=True, has_second=True):
                prev = None if first else Slot(s.n - 1, s.j - (1 - s.g), (s.phase + 3) % 4)
                nsums = NH * s.n
                mrows = NT * (s.n + 1)
                stats_done = None
                for u in range(UNITS):
                    scores_t(s, u)
                    if u == SUMS_AT and not first:
                        sums(prev, NH - 1, mrows)
                    if u == SUMS_AT + UNITS // NH:
                        sums(s, 0, mrows_now(s, u) if has_next else mrows)
                        nsums = nsums + 1
                    if (u - PV_LAG) % HG == 1 or HG == 1:
                        done = (u - PV_LAG - 1) // HG - 1
                        if done >= 0:
                            weighted_values(s, done // NT, done % NT)
                        elif not first:
                            weighted_values(prev, NH - 1, NT - 1)
                    if has_next:
                        for w in max_units_at(u):
                            scores_for_max(s.n + 1, 1 - s.qk, w)
                        if u in MAX_ROWS_AT:
                            max_rows(s.n + 1, MAX_ROWS_AT[u], nsums, stats_done)
                            stats_done = None
                    if s.g == 0 and not first and u in PROJ_AT:
                        piece = PROJ_AT.index(u)
                        j = s.j - 1
                        if piece == 0:
                            pe.wait_ge(qkl_done, 4 * (s.n + 1) + 4)
                            pe.wait_ge(norm_done, NH * s.n)
                        else:
                            pe.wait_ge(proj_done, 4 * j + piece)
                        project_out(piece)
                    if s.g == 0 and u == GN_AT and has_second:
                        group_stats(s.j + 1, mrows_now(s, u, True), nsums)
                        stats_done = s.j + 2
                    if s.g == 1 and has_second and u in V_AT:
                        r = V_AT.index(u)
                        if r == 0:
                            pe.wait_ge(qkl_done, 4 * (s.n + 1) + 4)
                        else:
                            pe.wait_ge(v_done, 4 * (s.j + 1) + r)
                        project_v(r)
                    if has_second and u in QK_AT:
                        r = QK_AT.index(u)
                        n2 = s.n + 2
                        if r == 0:
                            if s.g == 0:
                                pe.wait_ge(xn_done, CT * (s.j + 2))
                                if not first:
                                    pe.wait_ge(proj_done, 4 * s.j)
                            else:
                                pe.wait_ge(v_done, 4 * (s.j + 1) + 4)
                        else:
                            pe.wait_ge(qkl_done, 4 * n2 + r)
                        project_qk(n2, s.g, r)

            def mrows_now(s, u, with_u=False):
                return NT * (s.n + 1) + sum(1 for at in MAX_ROWS_AT if at < u + with_u)

            pe.wait_ge(loaded, 32)
            pe.wait_ge(const_dve, CONSTANTS)
            group_stats(0, 0, 0)
            pe.wait_ge(weights, 32)
            pe.wait_ge(wproj_loaded, 16)
            pe.wait_ge(xn_done, CT)
            for r in range(4):
                if r:
                    pe.wait_ge(qkl_done, r)
                project_qk(0, 0, r)
            for r in range(4):
                if r == 0:
                    pe.wait_ge(qkl_done, 4)
                else:
                    pe.wait_ge(v_done, r)
                project_v(r)
            for r in range(4):
                if r == 0:
                    pe.wait_ge(v_done, 4)
                else:
                    pe.wait_ge(qkl_done, 4 + r)
                project_qk(1, 1, r)
            for w in range(UNITS):
                scores_for_max(0, 0, w)
                if w % (HG * NH) == HG * NH - 1:
                    max_rows(0, w // (HG * NH), 0, 1)
            run_slots(pe, slot)
            last = plain(SLOTS - 1)
            weighted_values(last, NH - 1, NT - 1)
            sums(last, NH - 1, NT * SLOTS)
            for piece in range(CT * NH):
                j = BLOCKS - 1
                if piece == 0:
                    pe.wait_ge(norm_done, NH * SLOTS)
                    pe.wait_ge(proj_done, 4 * j)
                else:
                    pe.wait_ge(proj_done, 4 * j + piece)
                project_out(piece)

        @block.scalar
        def _(act):
            def exp(s, u):
                half_of, t, h = u // (NT * HG), u // HG % NT, u % HG
                half = NH * s.n + half_of
                started = not (isinstance(half, int) and half == 0 and t < 4)
                if h == 0 and started:
                    act.wait_ge(pv_done, NT * half + t - 3)
                    if t >= 4:
                        act.wait_ge(pool_added, ADDS * half + max(1, t - 4))
                    elif t + 4 < POOLED:
                        act.wait_ge(pool_added, ADDS * (half - 1) + t + 4)
                    else:
                        act.wait_ge(sum_ready, half)
                act.wait_ge(st_ready, UNITS * s.n + u + 1)
                act.activation(pt[t % 4][:, h, :], ps_t[u % 2][:, :], ACT.Exp, scale=SCALE).then_inc(exp_done, 1)

            def max_row(n, b, t):
                act.wait_ge(mrow_ready, NT * n + t + 1)
                act.activation(qs[b][MROW:MROW + 1, :, t * P:(t + 1) * P],
                               ps_a[MROW:MROW + 1, :].rearrange("p (h s) -> p h s", h=HG),
                               ACT.Identity).then_inc(mrow_done, 1)

            def qk_high(n, g, parity, r):
                which, hf = r // NH, r % NH
                if r == 0 and not (isinstance(n, int) and n == 0):
                    act.wait_ge(staged, 16 * STAGE_DMAS * n)
                act.wait_ge(qk_ready, 4 * n + r + 1)
                dst = stage["qh" if which == 0 else "kh"]
                act.activation(dst[:, hf * HALF:(hf + 1) * HALF], ps_d[:, :], ACT.Identity,
                               bias=par[:, parity, 4 + 2 * which + g:5 + 2 * which + g]).then_inc(qkh_done, 1)

            def group_stats_out(j):
                act.wait_ge(gm_ready, j + 1)
                act.activation(gm[:, :, :], ps_a[:, 0:2 * CT].rearrange("p (c k) -> p c k", c=CT),
                               ACT.Identity).then_inc(gm_done, 1)

            def normalise(j):
                act.wait_ge(gn_step, GN_STEPS * (j + 1))
                for ct in range(CT):
                    act.activation(xn[:, ct, :], xn[:, ct, :], ACT.Identity, scale=gn_a[:, ct:ct + 1],
                                   bias=gn_c[:, ct:ct + 1]).then_inc(xn_done, 1)

            def slot(s, first=False, has_next=True, has_second=True):
                for u in range(UNITS):
                    exp(s, u)
                    if has_next and u in MAX_ROWS_AT:
                        max_row(s.n + 1, 1 - s.qk, MAX_ROWS_AT[u])
                    if s.g == 0 and has_second and u == GN_AT:
                        group_stats_out(s.j + 1)
                    if s.g == 0 and has_second and u == GN_AT + 4:
                        normalise(s.j + 1)
                    if has_second and u in QK_AT:
                        qk_high(s.n + 2, s.g, 1 - s.v, QK_AT.index(u))

            group_stats_out(0)
            normalise(0)
            for r in range(4):
                qk_high(0, 0, 0, r)
            for r in range(4):
                qk_high(1, 1, 0, r)
            for t in range(NT):
                max_row(0, 0, t)
            run_slots(act, slot)

        @block.vector
        def _(dve):
            dve.memset(ones[:, :], 1.0).then_inc(const_dve, 1)
            dve.memset(neg_half[:, :], -0.5).then_inc(const_dve, 1)
            dve.memset(eps[:, :], EPS).then_inc(const_dve, 1)
            dve.memset(inv_count[:, :, :], QUARTERS / S).then_inc(const_dve, 1)
            for b in range(2):
                dve.memset(ks[b][MROW:MROW + 1, :, :].bitcast(F32), 1.0).then_inc(const_dve, 1)
                dve.memset(qs[b][MROW:MROW + 1, :, :].bitcast(F32), 0.0).then_inc(const_dve, 1)

            def max_unit(n, w):
                t, h, kf = w // (HG * NH), w // NH % HG, w % NH
                dve.wait_ge(sm_ready, UNITS * n + w + 1)
                if w % (HG * NH) == 0 and not (isinstance(n, int) and NT * n + t < 2):
                    dve.wait_ge(neg_done, NT * n + t - 1)
                dve.tensor_reduce(raw_max[:, t % 2, h, kf:kf + 1], ps_m[w % 2][:, :], AX.X, ALU.max)\
                   .then_inc(max_done, 1)
                if w % (HG * NH) == HG * NH - 1:
                    dve.wait_ge(max_done, UNITS * n + w + 1)
                    if not (isinstance(n, int) and NT * n + t < 2):
                        dve.wait_ge(mrow_ready, NT * n + t - 1)
                    dve.tensor_reduce(neg_max[:, t % 2, :], raw_max[:, t % 2, :, :], AX.X, ALU.max,
                                      negate=True).then_inc(neg_done, 1)

            def qk_low(n, g, parity, r):
                which, hf = r // NH, r % NH
                cols = slice(hf * HALF, (hf + 1) * HALF)
                hi, lo = (stage["qh"], stage["ql"]) if which == 0 else (stage["kh"], stage["kl"])
                dve.wait_ge(qkh_done, 4 * n + r + 1)
                dve.scalar_tensor_tensor(out=lo[:, cols], in0=ps_d[:, :],
                                         scalar=par[:, parity, 4 + 2 * which + g:5 + 2 * which + g],
                                         in1=hi[:, cols].bitcast(F32), op0=ALU.add,
                                         op1=ALU.subtract).then_inc(qkl_done, 1)

            def v_out(j, parity, r):
                dve.wait_ge(v_ready, 4 * j + r + 1)
                dve.tensor_tensor(v[parity][:, 2 * r:2 * r + 2, :], ps_d[:, :].rearrange("p (t c) -> p t c", t=2),
                                  bv[:, :].rearrange("p (t c) -> p t c", t=2), ALU.add).then_inc(v_done, 1)

            def channel_stats(j):
                dve.wait_ge(x_loaded, 48 * (j + 1))
                for ct in range(CT):
                    for hf in range(NH):
                        dve.bn_stats(stats[:, ct, hf, :], xn[:, ct, hf * HALF:(hf + 1) * HALF]).then_inc(bn_done, 1)

            def divide(half, g, hf):
                dve.wait_ge(sum_ready, half + 1)
                if not (isinstance(half, int) and half == 0):
                    dve.wait_ge(norm_done, half)
                dve.reciprocal(rden[:, :], ps_a[:, :]).then_inc(rden_done, 1)
                dve.wait_ge(pv_done, NT * half + NT)
                dve.wait_ge(rden_done, half + 1)
                dve.tensor_tensor(att[:, g, hf * HALF:(hf + 1) * HALF], ps_v[hf][:, :], rden[:, :],
                                  ALU.mult).then_inc(norm_done, 1)

            def project_out(j, piece):
                hf, ct = piece // CT, piece % CT
                if piece == 0:
                    dve.wait_ge(res_loaded, 48 * (j + 1))
                dve.wait_ge(proj_ready, 4 * j + piece + 1)
                r = res[:, NH * ct + hf, :]
                dve.scalar_tensor_tensor(out=r, in0=ps_d[:, :], scalar=bp[:, ct:ct + 1], in1=r,
                                         op0=ALU.add, op1=ALU.add).then_inc(proj_done, 1)

            def slot(s, first=False, has_next=True, has_second=True):
                for u in range(UNITS):
                    if u == SUMS_AT and not first:
                        divide(NH * s.n - 1, 1 - s.g, NH - 1)
                    if u == SUMS_AT + UNITS // NH:
                        if s.g == 0 and not first:
                            dve.wait_ge(proj_ready, 4 * s.j)
                        divide(NH * s.n, s.g, 0)
                    if has_next:
                        for w in max_units_at(u):
                            max_unit(s.n + 1, w)
                    if s.g == 0 and not first and u in PROJ_AT:
                        project_out(s.j - 1, PROJ_AT.index(u))
                    if s.g == 0 and has_second and u == GN_AT - 9:
                        channel_stats(s.j + 1)
                    if s.g == 1 and has_second and u in V_AT:
                        v_out(s.j + 1, 1 - s.v, V_AT.index(u))
                    if has_second and u in QK_AT:
                        qk_low(s.n + 2, s.g, 1 - s.v, QK_AT.index(u))

            channel_stats(0)
            for r in range(4):
                qk_low(0, 0, 0, r)
            dve.wait_ge(weights, 32)
            for r in range(4):
                v_out(0, 0, r)
            for r in range(4):
                qk_low(1, 1, 0, r)
            for w in range(UNITS):
                max_unit(0, w)
            run_slots(dve, slot)
            divide(NH * SLOTS - 1, 1, NH - 1)
            for piece in range(CT * NH):
                project_out(BLOCKS - 1, piece)

        @block.gpsimd
        def _(pool):
            def mean_square(j):
                pool.wait_ge(bn_done, CT * NH * (j + 1))
                parts = stats[:, :, :, :].rearrange("p c h (o k) -> p c (h o) k", o=2)
                mean, m2 = parts[:, :, :, 1], parts[:, :, :, 2]
                pool.tensor_tensor(sq4[:, :, :], mean, mean, ALU.mult).then_inc(mv_done, 1)
                pool.tensor_tensor(mv[:, :, :, 1], m2, inv_count[:, :, :], ALU.mult).then_inc(mv_done, 1)
                pool.tensor_copy(mv[:, :, :, 0], mean).then_inc(mv_done, 1)
                pool.wait_ge(mv_done, MV_STEPS * j + 3)
                pool.tensor_tensor(mv[:, :, :, 1], mv[:, :, :, 1], sq4[:, :, :], ALU.add).then_inc(mv_done, 1)

            def scale_and_shift(j, parity):
                pool.wait_ge(gm_done, j + 1)
                step = [0]

                def then(ins):
                    ins.then_inc(gn_step, 1)
                    step[0] += 1
                    pool.wait_ge(gn_step, GN_STEPS * j + step[0])

                then(pool.tensor_tensor(sq[:, :], gm[:, :, 0], gm[:, :, 0], ALU.mult))
                then(pool.tensor_tensor(var[:, :], gm[:, :, 1], sq[:, :], ALU.subtract))
                then(pool.tensor_tensor(var[:, :], var[:, :], eps[:, :], ALU.add))
                then(pool.tensor_tensor(rstd[:, :], var[:, :], neg_half[:, :], ALU.pow))
                then(pool.tensor_tensor(gn_a[:, :], rstd[:, :], par[:, parity, 0:2], ALU.mult))
                then(pool.tensor_tensor(sq[:, :], gm[:, :, 0], gn_a[:, :], ALU.mult))
                then(pool.tensor_tensor(gn_c[:, :], par[:, parity, 2:4], sq[:, :], ALU.subtract))

            def add(half, t):
                pool.wait_ge(exp_done, HG * (NT * half + t + 1))
                if t == 1:
                    if not (isinstance(half, int) and half == 0):
                        pool.wait_ge(sum_ready, half)
                    a = pt[0]
                else:
                    pool.wait_ge(pool_added, ADDS * half + t - 1)
                    a = acc
                pool.tensor_tensor(acc[:, :, :], a[:, :, :], pt[t % 4][:, :, :], ALU.add).then_inc(pool_added, 1)

            def slot(s, first=False, has_next=True, has_second=True):
                for hf in range(NH):
                    for t in range(1, POOLED):
                        add(NH * s.n + hf, t)
                        if s.g == 0 and has_second and hf == 0 and t == 2:
                            mean_square(s.j + 1)
                        if s.g == 0 and has_second and hf == 0 and t == 3:
                            scale_and_shift(s.j + 1, 1 - s.v)

            pool.wait_ge(const_dve, CONSTANTS)
            mean_square(0)
            scale_and_shift(0, 0)
            run_slots(pool, slot)


MV_STEPS = 4
GN_STEPS = 7
CONSTANTS = 8

_OUT = (B, C, 32, 32)


def kernel(x, L0_conv_gamma, L0_conv_beta, L0_conv_w_qkv, L0_conv_b_qkv, L0_conv_w_proj, L0_conv_b_proj,
           L1_conv_gn_w, L1_conv_gn_b, L1_conv_qkv_w, L1_conv_proj_w, L1_conv_proj_b):
    import concourse.bacc as bacc
    from concourse.bass_utils import run_bass_kernel_spmd

    def tiles(a):
        return np.ascontiguousarray(a.reshape(CT, P, -1).transpose(1, 0, 2))

    def qkv(w):
        return tiles(w.reshape(HEADS, 3, HD, C).transpose(3, 1, 0, 2).reshape(C, 3 * C))

    def columns(a):
        return a.reshape(CT, P).T

    no_bias = np.zeros(3 * C, np.float32)
    biases = [np.asarray(b).reshape(HEADS, 3, HD).transpose(1, 0, 2).reshape(3, C)
              for b in (L0_conv_b_qkv, no_bias)]
    norms = [(L0_conv_gamma, L0_conv_beta), (L1_conv_gn_w, L1_conv_gn_b)]
    arrays = {
        "x_dram": np.ascontiguousarray(np.asarray(x).reshape(B, CT, P, S)),
        "w_qkv_dram": np.stack([qkv(np.asarray(w)) for w in (L0_conv_w_qkv, L1_conv_qkv_w)]),
        "w_proj_dram": np.stack([tiles(np.asarray(w).T) for w in (L0_conv_w_proj, L1_conv_proj_w)]),
        "pars_dram": np.stack([np.concatenate([columns(np.asarray(a)) for a in (g, b, bias[0], bias[1])], axis=1)
                               for (g, b), bias in zip(norms, biases)]),
        "bias_v_dram": np.stack([np.ascontiguousarray(np.broadcast_to(np.tile(bias[2], HALF // C), (P, HALF)))
                                 for bias in biases]),
        "bias_proj_dram": np.stack([np.ascontiguousarray(columns(np.asarray(b)))
                                    for b in (L0_conv_b_proj, L1_conv_proj_b)]),
        "ident_dram": np.eye(P, dtype=np.float32),
        "group_dram": np.kron(np.eye(P * GROUPS // C), np.full((C // GROUPS,) * 2, GROUPS / C / QUARTERS)).astype(np.float32),
    }
    nc = bacc.Bacc("TRN2", target_bir_lowering=False, num_devices=1)
    args = [nc.dram_tensor(name, a.shape, F32, kind="ExternalInput").ap() for name, a in arrays.items()]
    out = nc.dram_tensor("out_dram", [B, CT, P, S], F32, kind="ExternalOutput").ap()
    attention_layers(nc, *args, out)
    r = run_bass_kernel_spmd(nc, [arrays], core_ids=[0])
    return r.results[0]["out_dram"].reshape(_OUT)
```

```python
from contextlib import ExitStack

import numpy as np

import concourse.bass as bass
from concourse import mybir

F32 = mybir.dt.float32
F32R = mybir.dt.float32r
ALU = mybir.AluOpType
ACT = mybir.ActivationFunctionType
AX = mybir.AxisListType

LAYERS, B, C, S = 2, 8, 256, 1024
HEADS, GROUPS = 8, 32
EPS = 1e-5
HD = C // HEADS
SCALE = float(HD) ** -0.5
P = 128
CT = C // P
HG = HEADS // CT
NT = S // P
HALF = 512
NH = S // HALF
BLOCKS = LAYERS * B
SLOTS = BLOCKS * CT
UNITS = NH * NT * HG
KROWS = 3 * HD
MROW = KROWS
POOLED = 7
ADDS = POOLED - 1
QUARTERS = 2 * NH
STAGE_DMAS = 2 * 3
MAX_BANKS = 3
MAX_GROUP = HG * NH
LATER = 1
PV_AT = 3
SUMS_AT = 7
MAX_FROM, MAX_TO = 4, 62
FIRST_AT = (12, 17, 22, 27)
QK_AT = (33, 40, 47, 54)
STEP = 2
GN_AT = 23
LOOP_FROM, LOOP_SLOTS = 1, 4
LOOPS = (SLOTS - 4) // LOOP_SLOTS


class Slot:

    def __init__(self, n, j, phase):
        self.n, self.j = n, j
        self.g = phase % 2
        self.qk = phase % 2
        self.v = (phase // 2) % 2
        self.phase = phase


def plain(n):
    return Slot(n, n // 2, n % 4)


def looped(i, k):
    return Slot(LOOP_SLOTS * i + LOOP_FROM + k, 2 * i + (LOOP_FROM + k) // 2, (LOOP_FROM + k) % 4)


def run_slots(eng, slot):
    slot(plain(0), first=True)
    with eng.Fori(0, LOOPS) as i:
        for k in range(LOOP_SLOTS):
            slot(looped(i, k))
    for n in range(LOOP_FROM + LOOPS * LOOP_SLOTS, SLOTS):
        slot(plain(n), has_next=n + 1 < SLOTS, has_second=n + 2 < SLOTS)


def max_units_at(u):
    if not MAX_FROM <= u < MAX_TO:
        return range(0)
    span = MAX_TO - MAX_FROM
    return range((u - MAX_FROM) * UNITS // span, (u - MAX_FROM + 1) * UNITS // span)


MAX_ROWS_AT = {}
for _e in range(NT):
    _u = next(u for u in range(UNITS) if (_e + 1) * MAX_GROUP - 1 in max_units_at(u))
    MAX_ROWS_AT[min(_u + 2, UNITS - 1)] = _e


def attention_layers(nc, x, w_qkv, w_proj, pars, bias_v, bias_proj, ident_in, group_in, out):
    nc.disable_value_cache = True
    ctx = ExitStack()
    with ctx:
        def sb(name, shape, dt=F32):
            return ctx.enter_context(nc.sbuf_tensor(name, shape, dt))

        def bank(name):
            return ctx.enter_context(nc.psum_tensor(name, [P, HALF], F32))

        def sem(name):
            return ctx.enter_context(nc.semaphore(name))

        between = nc.dram_tensor("between", [B, CT, P, S], F32).ap()

        wq = sb("wq", [P, CT, 3 * C])
        wp = sb("wp", [P, CT, C])
        bv = sb("bv", [P, HALF])
        par = sb("par", [P, 2, 8])
        bp = sb("bp", [P, CT])
        ident = sb("ident", [P, P])
        group = sb("group", [P, P])
        ones = sb("ones", [P, HD])
        eps = sb("eps", [P, CT])
        neg_half = sb("neg_half", [P, CT])
        xn = sb("xn", [P, CT, S])
        stats = sb("stats", [P, CT, NH, 6])
        mv = sb("mv", [P, CT, QUARTERS, 2])
        sq4 = sb("sq4", [P, CT, QUARTERS])
        inv_count = sb("inv_count", [P, CT, QUARTERS])
        sq = sb("sq", [P, CT])
        gm = sb("gm", [P, CT, 2])
        var = sb("var", [P, CT])
        rstd = sb("rstd", [P, CT])
        gn_a = sb("gn_a", [P, CT])
        gn_c = sb("gn_c", [P, CT])
        stage = {w: sb("stage_" + w, [P, S], F32R) for w in ("qh", "ql", "kh", "kl")}
        qs = [sb(f"qs{b}", [P, HG, S], F32R) for b in range(2)]
        ks = [sb(f"ks{b}", [P, HG, S], F32R) for b in range(2)]
        v = [sb(f"v{b}", [P, NT, C]) for b in range(2)]
        pt = [sb(f"pt{b}", [P, HG, HALF]) for b in range(4)]
        acc = [sb(f"acc{b}", [P, HG, HALF]) for b in range(NH)]
        raw_max = sb("raw_max", [P, 2, NT // NH, NH])
        neg_max = sb("neg_max", [P, 2, NT // NH])
        raw = sb("raw", [P, HALF])
        turned = sb("turned", [P, HALF])
        rden = sb("rden", [P, HALF // HD])
        att = sb("att", [P, CT, S])
        res = sb("res", [P, CT * NH, HALF])

        ps_t = [bank(f"ps_t{b}") for b in range(2)]
        ps_m = [bank(f"ps_m{b}") for b in range(MAX_BANKS)]
        ps_v = bank("ps_v")
        ps_d = bank("ps_d")
        ps_a = bank("ps_a")

        loaded = sem("constants_loaded")
        weights = sem("weights_loaded")
        wproj_loaded = sem("wproj_loaded")
        x_loaded = sem("x_loaded")
        res_loaded = sem("res_loaded")
        stored = sem("stored")
        staged = [sem(f"staged_head{h}") for h in range(HG)]
        const_dve = sem("const_dve")
        bn_done = sem("bn_done")
        mv_done = sem("mv_done")
        gm_ready = sem("gm_ready")
        gm_done = sem("gm_done")
        gn_step = sem("gn_step")
        xn_done = sem("xn_done")
        qk_ready = sem("qk_ready")
        qkh_done = sem("qkh_done")
        qkl_done = sem("qkl_done")
        v_ready = sem("v_ready")
        v_done = sem("v_done")
        proj_ready = sem("proj_ready")
        proj_done = sem("proj_done")
        sm_ready = sem("sm_ready")
        max_done = sem("max_done")
        neg_done = sem("neg_done")
        mrow_ready = sem("mrow_ready")
        mrow_done = sem("mrow_done")
        st_ready = sem("st_ready")
        exp_done = sem("exp_done")
        pv_done = sem("pv_done")
        pool_added = sem("pool_added")
        sum_ready = sem("sum_ready")
        raw_done = sem("raw_done")
        divide_step = sem("divide_step")
        norm_done = sem("norm_done")

        block = ctx.enter_context(nc.Block())

        @block.sync
        def _(sp):
            sp.dma_start(ident[:, :], ident_in).then_inc(loaded, 16)
            sp.dma_start(group[:, :], group_in).then_inc(loaded, 16)

            def load_block(layer, src, image, parity):
                for ct in range(CT):
                    sp.dma_start(xn[:, ct, :], src[image, ct]).then_inc(x_loaded, 16)
                sp.dma_start(par[:, parity, :], pars[layer]).then_inc(x_loaded, 16)

            def load_weights(layer):
                sp.dma_start(wq[:, :, :], w_qkv[layer]).then_inc(weights, 16)
                sp.dma_start(bv[:, :], bias_v[layer]).then_inc(weights, 16)

            def load_residual(layer, src, image):
                for ct in range(CT):
                    sp.dma_start(res[:, NH * ct:NH * ct + NH, :],
                                 src[image, ct].rearrange("p (h s) -> p h s", h=NH)).then_inc(res_loaded, 16)
                sp.dma_start(bp[:, :], bias_proj[layer]).then_inc(res_loaded, 16)

            def store_block(dst, j, image):
                for piece in range(CT * NH):
                    sp.wait_ge(proj_done, CT * NH * j + piece + 1)
                    h, ct = piece // CT, piece % CT
                    sp.dma_start(dst[image, ct][:, h * HALF:(h + 1) * HALF],
                                 res[:, NH * ct + h, :]).then_inc(stored, 16)

            def stage_slot(n, b):
                sp.wait_ge(qkl_done, 4 * n + 4)
                for h in range(HG):
                    for dst, parts in ((ks[b], ("kh", "kl", "kh")), (qs[b], ("qh", "qh", "ql"))):
                        for r, part in enumerate(parts):
                            sp.dma_start(dst[HD * r:HD * (r + 1), h, :].bitcast(F32),
                                         stage[part][HD * h:HD * (h + 1), :].bitcast(F32)).then_inc(staged[h], 16)

            load_weights(0)
            load_block(0, x, 0, 0)
            sp.dma_start(wp[:, :, :], w_proj[0]).then_inc(wproj_loaded, 16)
            stage_slot(0, 0)
            stage_slot(1, 1)
            sp.wait_ge(qk_ready, 8)
            load_block(0, x, 1, 1)

            def body(i, next_layer, done_layer):
                nsrc = x if next_layer == 0 else between
                dsrc, ddst = (x, between) if done_layer == 0 else (between, out)
                for k in range(LOOP_SLOTS):
                    s = looped(i, k)
                    sp.wait_ge(st_ready, UNITS * s.n)
                    stage_slot(s.n + 1, 1 - s.qk)
                    if s.g == 1:
                        continue
                    sp.wait_ge(qk_ready, 4 * (2 * s.j + 2))
                    if isinstance(i, int) and s.j == B - 1:
                        sp.wait_ge(v_done, 4 * B)
                        load_weights(1)
                        sp.wait_ge(weights, 64)
                    load_block(next_layer, nsrc, s.j + 1 - B * next_layer, 1 - s.v)
                    if not (isinstance(s.j, int) and s.j < 2):
                        sp.wait_ge(stored, 16 * CT * NH * (s.j - 1))
                    load_residual(done_layer, dsrc, s.j - 1 - B * done_layer)
                    store_block(ddst, s.j - 1, s.j - 1 - B * done_layer)
                    if isinstance(i, int) and s.j == B:
                        sp.dma_start(wp[:, :, :], w_proj[1]).then_inc(wproj_loaded, 16)
                        sp.wait_ge(wproj_loaded, 32)

            turn = B // 2 - 1
            body(0, 0, 0)
            with sp.Fori(1, turn) as i:
                body(i, 0, 0)
            body(turn, 1, 0)
            with sp.Fori(turn + 1, LOOPS) as i:
                body(i, 1, 1)
            for n in range(LOOP_FROM + LOOPS * LOOP_SLOTS, SLOTS):
                s = plain(n)
                if n + 1 < SLOTS:
                    sp.wait_ge(st_ready, UNITS * n)
                    stage_slot(n + 1, 1 - s.qk)
                if s.g == 0:
                    sp.wait_ge(stored, 16 * CT * NH * (s.j - 1))
                    load_residual(1, between, s.j - 1 - B)
                    store_block(out, s.j - 1, s.j - 1 - B)
            sp.wait_ge(stored, 16 * CT * NH * (BLOCKS - 1))
            load_residual(1, between, B - 1)
            store_block(out, BLOCKS - 1, B - 1)
            sp.wait_ge(stored, 16 * CT * NH * BLOCKS)

        @block.tensor
        def _(pe):
            def aux_free(mrows, sums, stats_done=None):
                if not (isinstance(mrows, int) and mrows == 0):
                    pe.wait_ge(mrow_done, mrows)
                if not (isinstance(sums, int) and sums == 0):
                    pe.wait_ge(norm_done, sums)
                if stats_done is not None:
                    pe.wait_ge(gm_done, stats_done)

            def scores_t(s, u):
                hf, t, h = u // (NT * HG), u // HG % NT, u % HG
                if not (isinstance(s.n, int) and UNITS * s.n + u < 2):
                    pe.wait_ge(exp_done, UNITS * s.n + u - 1)
                if t == 0:
                    pe.wait_ge(mrow_done, NT * s.n + NH * h + hf + 1)
                pe.matmul(ps_t[u % 2][:, :], ks[s.qk][0:KROWS + 1, h, t * P:(t + 1) * P],
                          qs[s.qk][0:KROWS + 1, h, hf * HALF:(hf + 1) * HALF],
                          start=True, stop=True).then_inc(st_ready, 1)

            def scores_for_max(n, b, w):
                h, t, kf = w // (NT * NH), w // NH % NT, w % NH
                if w % (NT * NH) == 0:
                    pe.wait_ge(staged[h], 16 * STAGE_DMAS * (n + 1))
                if w >= MAX_BANKS:
                    pe.wait_ge(max_done, UNITS * n + w - MAX_BANKS + 1)
                elif not (isinstance(n, int) and n == 0):
                    last = max(x for x in range(UNITS) if x % MAX_BANKS == w)
                    pe.wait_ge(max_done, UNITS * (n - 1) + last + 1)
                pe.matmul(ps_m[w % MAX_BANKS][:, :], qs[b][0:KROWS, h, t * P:(t + 1) * P],
                          ks[b][0:KROWS, h, kf * HALF:(kf + 1) * HALF],
                          start=True, stop=True).then_inc(sm_ready, 1)

            def max_rows(n, e, sums, stats_done=None):
                pe.wait_ge(neg_done, NT * n + e + 1)
                aux_free(NT * n + e, sums, stats_done)
                for t in range(NT // NH):
                    mm = pe.matmul(ps_a[MROW:MROW + 1, t * P:(t + 1) * P], neg_max[:, e % 2, t:t + 1],
                                   ident[:, :], start=True, stop=True)
                mm.then_inc(mrow_ready, 1)

            def weighted_values(s, hf, t):
                half = NH * s.n + hf
                pe.wait_ge(exp_done, HG * (NT * half + t + 1))
                if t == 0:
                    if not (isinstance(half, int) and half == 0):
                        pe.wait_ge(raw_done, half)
                    if hf == 0:
                        pe.wait_ge(v_done, 4 * s.j + 4)
                for h in range(HG):
                    c = (s.g * HG + h) * HD
                    mm = pe.matmul(ps_v[HD * h:HD * (h + 1), :], v[s.v][:, t, c:c + HD],
                                   pt[t % 4][:, h, :], start=(t == 0), stop=(t == NT - 1))
                mm.then_inc(pv_done, 1)

            def sums(s, hf, mrows):
                half = NH * s.n + hf
                pe.wait_ge(pool_added, ADDS * half + ADDS)
                aux_free(mrows, half)
                tiles = [pt[t % 4] for t in range(POOLED, NT)] + [acc[hf]]
                for k, tile in enumerate(tiles):
                    for h in range(HG):
                        mm = pe.matmul(ps_a[HD * h:HD * (h + 1), :], ones[:, :], tile[:, h, :],
                                       start=(k == 0), stop=(k == len(tiles) - 1))
                mm.then_inc(sum_ready, 1)

            def project_qk(g, r, kt):
                which, hf = r // NH, r % NH
                c = which * C + g * P
                mm = pe.matmul(ps_d[:, :], wq[:, kt, c:c + P], xn[:, kt, hf * HALF:(hf + 1) * HALF],
                               start=(kt == 0), stop=(kt == CT - 1))
                if kt == CT - 1:
                    mm.then_inc(qk_ready, 1)

            def project_v(r, t):
                for kt in range(CT):
                    mm = pe.matmul(ps_d[:, t * C:(t + 1) * C], xn[:, kt, (2 * r + t) * P:(2 * r + t + 1) * P],
                                   wq[:, kt, 2 * C:3 * C], start=(kt == 0), stop=(kt == CT - 1))
                if t == 1:
                    mm.then_inc(v_ready, 1)

            def project_out(piece, kt):
                hf, ct = piece // CT, piece % CT
                mm = pe.matmul(ps_d[:, :], wp[:, kt, ct * P:(ct + 1) * P],
                               att[:, kt, hf * HALF:(hf + 1) * HALF], start=(kt == 0), stop=(kt == CT - 1))
                if kt == CT - 1:
                    mm.then_inc(proj_ready, 1)

            def group_stats(j, mrows, nsums):
                pe.wait_ge(mv_done, MV_STEPS * (j + 1))
                aux_free(mrows, nsums)
                for quarter in range(QUARTERS):
                    mm = pe.matmul(ps_a[:, 0:2 * CT], group[:, :], mv[:, :, quarter, :],
                                   start=(quarter == 0), stop=(quarter == QUARTERS - 1))
                mm.then_inc(gm_ready, 1)

            def slot(s, first=False, has_next=True, has_second=True):
                prev = None if first else Slot(s.n - 1, s.j - (1 - s.g), (s.phase + 3) % 4)
                nsums = NH * s.n
                mrows = NT * (s.n + 1)
                stats_done = None
                for u in range(UNITS):
                    scores_t(s, u)
                    if u == SUMS_AT and not first:
                        sums(prev, NH - 1, mrows)
                    if u == SUMS_AT + UNITS // NH:
                        sums(s, 0, mrows_now(s, u) if has_next else mrows)
                        nsums = nsums + 1
                    if u % HG == PV_AT:
                        done = u // HG - 1
                        if done >= 0:
                            weighted_values(s, done // NT, done % NT)
                        elif not first:
                            weighted_values(prev, NH - 1, NT - 1)
                    if has_next:
                        for w in max_units_at(u):
                            scores_for_max(s.n + 1, 1 - s.qk, w)
                        if u in MAX_ROWS_AT:
                            max_rows(s.n + 1, MAX_ROWS_AT[u], nsums, stats_done)
                            stats_done = None
                    if s.g == 0 and has_second and u == GN_AT:
                        group_stats(s.j + 1, mrows_now(s, u, True), nsums)
                        stats_done = s.j + 2
                    if s.g == 0 and not first and u in FIRST_AT:
                        piece = FIRST_AT.index(u)
                        j = s.j - 1
                        if piece == 0:
                            pe.wait_ge(qkl_done, 4 * (s.n + 1) + 4)
                            pe.wait_ge(norm_done, NH * s.n)
                        else:
                            pe.wait_ge(proj_done, 4 * j + piece)
                        project_out(piece, 0)
                    if s.g == 0 and not first and u - STEP in FIRST_AT:
                        project_out(FIRST_AT.index(u - STEP), 1)
                    if s.g == 1 and has_second and u in FIRST_AT:
                        r = FIRST_AT.index(u)
                        if r == 0:
                            pe.wait_ge(qkl_done, 4 * (s.n + 1) + 4)
                        else:
                            pe.wait_ge(v_done, 4 * (s.j + 1) + r)
                        project_v(r, 0)
                    if s.g == 1 and has_second and u - STEP in FIRST_AT:
                        project_v(FIRST_AT.index(u - STEP), 1)
                    if has_second and u in QK_AT:
                        r = QK_AT.index(u)
                        if r == 0:
                            if s.g == 0:
                                pe.wait_ge(xn_done, CT * (s.j + 2))
                                if not first:
                                    pe.wait_ge(proj_done, 4 * s.j)
                            else:
                                pe.wait_ge(v_done, 4 * (s.j + 1) + 4)
                        else:
                            pe.wait_ge(qkl_done, 4 * (s.n + 2) + r)
                        project_qk(s.g, r, 0)
                    if has_second and u - STEP in QK_AT:
                        project_qk(s.g, QK_AT.index(u - STEP), 1)

            def mrows_now(s, u, with_u=False):
                return NT * (s.n + 1) + sum(1 for at in MAX_ROWS_AT if at < u + with_u)

            pe.wait_ge(loaded, 32)
            pe.wait_ge(const_dve, CONSTANTS)
            group_stats(0, 0, 0)
            pe.wait_ge(weights, 32)
            pe.wait_ge(wproj_loaded, 16)
            pe.wait_ge(xn_done, CT)
            for r in range(4):
                if r:
                    pe.wait_ge(qkl_done, r)
                for kt in range(CT):
                    project_qk(0, r, kt)
            for r in range(4):
                if r == 0:
                    pe.wait_ge(qkl_done, 4)
                else:
                    pe.wait_ge(v_done, r)
                for t in range(2):
                    project_v(r, t)
            for r in range(4):
                if r == 0:
                    pe.wait_ge(v_done, 4)
                else:
                    pe.wait_ge(qkl_done, 4 + r)
                for kt in range(CT):
                    project_qk(1, r, kt)
            for w in range(UNITS):
                scores_for_max(0, 0, w)
                if w % MAX_GROUP == MAX_GROUP - 1:
                    max_rows(0, w // MAX_GROUP, 0, 1)
            run_slots(pe, slot)
            last = plain(SLOTS - 1)
            weighted_values(last, NH - 1, NT - 1)
            sums(last, NH - 1, NT * SLOTS)
            for piece in range(CT * NH):
                j = BLOCKS - 1
                if piece == 0:
                    pe.wait_ge(norm_done, NH * SLOTS)
                    pe.wait_ge(proj_done, 4 * j)
                else:
                    pe.wait_ge(proj_done, 4 * j + piece)
                for kt in range(CT):
                    project_out(piece, kt)

        @block.scalar
        def _(act):
            def exp(s, u):
                half_of, t, h = u // (NT * HG), u // HG % NT, u % HG
                half = NH * s.n + half_of
                started = not (isinstance(half, int) and half == 0 and t < 4)
                if h == 0 and started:
                    act.wait_ge(pv_done, NT * half + t - 3)
                    if t >= 4:
                        act.wait_ge(pool_added, ADDS * half + max(1, t - 4))
                    elif t + 4 < POOLED:
                        act.wait_ge(pool_added, ADDS * (half - 1) + t + 4)
                    else:
                        act.wait_ge(sum_ready, half)
                act.wait_ge(st_ready, UNITS * s.n + u + 1)
                act.activation(pt[t % 4][:, h, :], ps_t[u % 2][:, :], ACT.Exp, scale=SCALE).then_inc(exp_done, 1)

            def max_row(n, b, e):
                h, hf = e // NH, e % NH
                act.wait_ge(mrow_ready, NT * n + e + 1)
                act.activation(qs[b][MROW:MROW + 1, h, hf * HALF:(hf + 1) * HALF], ps_a[MROW:MROW + 1, :],
                               ACT.Identity).then_inc(mrow_done, 1)

            def values_out(half):
                act.wait_ge(pv_done, NT * half + NT)
                if not (isinstance(half, int) and half == 0):
                    act.wait_ge(norm_done, half)
                act.activation(raw[:, :], ps_v[:, :], ACT.Identity).then_inc(raw_done, 1)

            def qk_high(n, g, parity, r):
                which, hf = r // NH, r % NH
                if r == 0 and not (isinstance(n, int) and n == 0):
                    for h in range(HG):
                        act.wait_ge(staged[h], 16 * STAGE_DMAS * n)
                act.wait_ge(qk_ready, 4 * n + r + 1)
                dst = stage["qh" if which == 0 else "kh"]
                act.activation(dst[:, hf * HALF:(hf + 1) * HALF], ps_d[:, :], ACT.Identity,
                               bias=par[:, parity, 4 + 2 * which + g:5 + 2 * which + g]).then_inc(qkh_done, 1)

            def group_stats_out(j):
                act.wait_ge(gm_ready, j + 1)
                act.activation(gm[:, :, :], ps_a[:, 0:2 * CT].rearrange("p (c k) -> p c k", c=CT),
                               ACT.Identity).then_inc(gm_done, 1)

            def normalise(j):
                act.wait_ge(gn_step, GN_STEPS * (j + 1))
                for ct in range(CT):
                    act.activation(xn[:, ct, :], xn[:, ct, :], ACT.Identity, scale=gn_a[:, ct:ct + 1],
                                   bias=gn_c[:, ct:ct + 1]).then_inc(xn_done, 1)

            def slot(s, first=False, has_next=True, has_second=True):
                for u in range(UNITS):
                    exp(s, u)
                    if u == PV_AT + LATER and not first:
                        values_out(NH * s.n - 1)
                    if u == PV_AT + LATER + UNITS // NH:
                        values_out(NH * s.n)
                    for at, e in MAX_ROWS_AT.items():
                        if has_next and u == min(at + LATER, UNITS - 1):
                            max_row(s.n + 1, 1 - s.qk, e)
                    if s.g == 0 and has_second and u == GN_AT + LATER:
                        group_stats_out(s.j + 1)
                    if s.g == 0 and has_second and u == GN_AT + 4:
                        normalise(s.j + 1)
                    if has_second and u - STEP - LATER in QK_AT:
                        qk_high(s.n + 2, s.g, 1 - s.v, QK_AT.index(u - STEP - LATER))

            group_stats_out(0)
            normalise(0)
            for r in range(4):
                qk_high(0, 0, 0, r)
            for r in range(4):
                qk_high(1, 1, 0, r)
            for e in range(NT):
                max_row(0, 0, e)
            run_slots(act, slot)
            values_out(NH * SLOTS - 1)

        @block.vector
        def _(dve):
            dve.memset(ones[:, :], 1.0).then_inc(const_dve, 1)
            dve.memset(neg_half[:, :], -0.5).then_inc(const_dve, 1)
            dve.memset(eps[:, :], EPS).then_inc(const_dve, 1)
            dve.memset(inv_count[:, :, :], QUARTERS / S).then_inc(const_dve, 1)
            for b in range(2):
                dve.memset(ks[b][MROW:MROW + 1, :, :].bitcast(F32), 1.0).then_inc(const_dve, 1)
                dve.memset(qs[b][MROW:MROW + 1, :, :].bitcast(F32), 0.0).then_inc(const_dve, 1)

            def max_unit(n, w):
                e, t, kf = w // MAX_GROUP, w // NH % (NT // NH), w % NH
                dve.wait_ge(sm_ready, UNITS * n + w + 1)
                if w % MAX_GROUP == 0 and not (isinstance(n, int) and NT * n + e < 2):
                    dve.wait_ge(neg_done, NT * n + e - 1)
                dve.tensor_reduce(raw_max[:, e % 2, t, kf:kf + 1], ps_m[w % MAX_BANKS][:, :], AX.X, ALU.max)\
                   .then_inc(max_done, 1)
                if w % MAX_GROUP == MAX_GROUP - 1:
                    dve.wait_ge(max_done, UNITS * n + w + 1)
                    if not (isinstance(n, int) and NT * n + e < 2):
                        dve.wait_ge(mrow_ready, NT * n + e - 1)
                    dve.tensor_reduce(neg_max[:, e % 2, :], raw_max[:, e % 2, :, :], AX.X, ALU.max,
                                      negate=True).then_inc(neg_done, 1)

            def qk_low(n, g, parity, r):
                which, hf = r // NH, r % NH
                cols = slice(hf * HALF, (hf + 1) * HALF)
                hi, lo = (stage["qh"], stage["ql"]) if which == 0 else (stage["kh"], stage["kl"])
                dve.wait_ge(qkh_done, 4 * n + r + 1)
                dve.scalar_tensor_tensor(out=lo[:, cols], in0=ps_d[:, :],
                                         scalar=par[:, parity, 4 + 2 * which + g:5 + 2 * which + g],
                                         in1=hi[:, cols].bitcast(F32), op0=ALU.add,
                                         op1=ALU.subtract).then_inc(qkl_done, 1)

            def v_out(j, parity, r):
                dve.wait_ge(v_ready, 4 * j + r + 1)
                dve.tensor_tensor(v[parity][:, 2 * r:2 * r + 2, :], ps_d[:, :].rearrange("p (t c) -> p t c", t=2),
                                  bv[:, :].rearrange("p (t c) -> p t c", t=2), ALU.add).then_inc(v_done, 1)

            def channel_stats(j):
                dve.wait_ge(x_loaded, 48 * (j + 1))
                for ct in range(CT):
                    for hf in range(NH):
                        dve.bn_stats(stats[:, ct, hf, :], xn[:, ct, hf * HALF:(hf + 1) * HALF]).then_inc(bn_done, 1)

            def divide(half, g, hf):
                dve.wait_ge(sum_ready, half + 1)
                dve.transpose(turned[:, :], ps_a[:, :]).then_inc(divide_step, 1)
                dve.wait_ge(divide_step, 3 * half + 1)
                dve.reciprocal(rden[:, :], turned[:, 0:HALF:HD]).then_inc(divide_step, 1)
                dve.wait_ge(divide_step, 3 * half + 2)
                dve.transpose(ps_a[:, :], rden[:, :].unsqueeze(2).to_broadcast([P, HALF // HD, HD]))\
                   .then_inc(divide_step, 1)
                dve.wait_ge(raw_done, half + 1)
                dve.wait_ge(divide_step, 3 * half + 3)
                dve.tensor_tensor(att[:, g, hf * HALF:(hf + 1) * HALF], raw[:, :], ps_a[:, :],
                                  ALU.mult).then_inc(norm_done, 1)

            def project_out(j, piece):
                hf, ct = piece // CT, piece % CT
                if piece == 0:
                    dve.wait_ge(res_loaded, 48 * (j + 1))
                dve.wait_ge(proj_ready, 4 * j + piece + 1)
                r = res[:, NH * ct + hf, :]
                dve.scalar_tensor_tensor(out=r, in0=ps_d[:, :], scalar=bp[:, ct:ct + 1], in1=r,
                                         op0=ALU.add, op1=ALU.add).then_inc(proj_done, 1)

            def slot(s, first=False, has_next=True, has_second=True):
                for u in range(UNITS):
                    if u == SUMS_AT + LATER and not first:
                        divide(NH * s.n - 1, 1 - s.g, NH - 1)
                    if u == SUMS_AT + LATER + UNITS // NH:
                        if s.g == 0 and not first:
                            dve.wait_ge(proj_ready, 4 * s.j)
                        divide(NH * s.n, s.g, 0)
                    if has_next:
                        for w in max_units_at(u):
                            max_unit(s.n + 1, w)
                    if s.g == 0 and not first and u - STEP - LATER in FIRST_AT:
                        project_out(s.j - 1, FIRST_AT.index(u - STEP - LATER))
                    if s.g == 0 and has_second and u == GN_AT - 8:
                        channel_stats(s.j + 1)
                    if s.g == 1 and has_second and u - STEP - LATER in FIRST_AT:
                        v_out(s.j + 1, 1 - s.v, FIRST_AT.index(u - STEP - LATER))
                    if has_second and u - STEP - 2 * LATER in QK_AT:
                        qk_low(s.n + 2, s.g, 1 - s.v, QK_AT.index(u - STEP - 2 * LATER))

            channel_stats(0)
            for r in range(4):
                qk_low(0, 0, 0, r)
            dve.wait_ge(weights, 32)
            for r in range(4):
                v_out(0, 0, r)
            for r in range(4):
                qk_low(1, 1, 0, r)
            for w in range(UNITS):
                max_unit(0, w)
            run_slots(dve, slot)
            divide(NH * SLOTS - 1, 1, NH - 1)
            for piece in range(CT * NH):
                project_out(BLOCKS - 1, piece)

        @block.gpsimd
        def _(pool):
            def mean_square(j):
                pool.wait_ge(bn_done, CT * NH * (j + 1))
                parts = stats[:, :, :, :].rearrange("p c h (o k) -> p c (h o) k", o=2)
                mean, m2 = parts[:, :, :, 1], parts[:, :, :, 2]
                pool.tensor_tensor(sq4[:, :, :], mean, mean, ALU.mult).then_inc(mv_done, 1)
                pool.tensor_tensor(mv[:, :, :, 1], m2, inv_count[:, :, :], ALU.mult).then_inc(mv_done, 1)
                pool.tensor_copy(mv[:, :, :, 0], mean).then_inc(mv_done, 1)
                pool.wait_ge(mv_done, MV_STEPS * j + 3)
                pool.tensor_tensor(mv[:, :, :, 1], mv[:, :, :, 1], sq4[:, :, :], ALU.add).then_inc(mv_done, 1)

            def scale_and_shift(j, parity):
                pool.wait_ge(gm_done, j + 1)
                step = [0]

                def then(ins):
                    ins.then_inc(gn_step, 1)
                    step[0] += 1
                    pool.wait_ge(gn_step, GN_STEPS * j + step[0])

                then(pool.tensor_tensor(sq[:, :], gm[:, :, 0], gm[:, :, 0], ALU.mult))
                then(pool.tensor_tensor(var[:, :], gm[:, :, 1], sq[:, :], ALU.subtract))
                then(pool.tensor_tensor(var[:, :], var[:, :], eps[:, :], ALU.add))
                then(pool.tensor_tensor(rstd[:, :], var[:, :], neg_half[:, :], ALU.pow))
                then(pool.tensor_tensor(gn_a[:, :], rstd[:, :], par[:, parity, 0:2], ALU.mult))
                then(pool.tensor_tensor(sq[:, :], gm[:, :, 0], gn_a[:, :], ALU.mult))
                then(pool.tensor_tensor(gn_c[:, :], par[:, parity, 2:4], sq[:, :], ALU.subtract))

            def add(half, hf, t):
                pool.wait_ge(exp_done, HG * (NT * half + t + 1))
                if t == 1:
                    if not (isinstance(half, int) and half < NH):
                        pool.wait_ge(sum_ready, half - 1)
                    a = pt[0]
                else:
                    pool.wait_ge(pool_added, ADDS * half + t - 1)
                    a = acc[hf]
                pool.tensor_tensor(acc[hf][:, :, :], a[:, :, :], pt[t % 4][:, :, :], ALU.add).then_inc(pool_added, 1)

            def slot(s, first=False, has_next=True, has_second=True):
                for hf in range(NH):
                    for t in range(1, POOLED):
                        add(NH * s.n + hf, hf, t)
                        if s.g == 0 and has_second and hf == 0 and t == 2:
                            mean_square(s.j + 1)
                        if s.g == 0 and has_second and hf == 0 and t == 3:
                            scale_and_shift(s.j + 1, 1 - s.v)

            pool.wait_ge(const_dve, CONSTANTS)
            mean_square(0)
            scale_and_shift(0, 0)
            run_slots(pool, slot)


MV_STEPS = 4
GN_STEPS = 7
CONSTANTS = 8

_OUT = (B, C, 32, 32)


def kernel(x, L0_conv_gamma, L0_conv_beta, L0_conv_w_qkv, L0_conv_b_qkv, L0_conv_w_proj, L0_conv_b_proj,
           L1_conv_gn_w, L1_conv_gn_b, L1_conv_qkv_w, L1_conv_proj_w, L1_conv_proj_b):
    import concourse.bacc as bacc
    from concourse.bass_utils import run_bass_kernel_spmd

    def tiles(a):
        return np.ascontiguousarray(a.reshape(CT, P, -1).transpose(1, 0, 2))

    def qkv(w):
        return tiles(w.reshape(HEADS, 3, HD, C).transpose(3, 1, 0, 2).reshape(C, 3 * C))

    def columns(a):
        return a.reshape(CT, P).T

    no_bias = np.zeros(3 * C, np.float32)
    biases = [np.asarray(b).reshape(HEADS, 3, HD).transpose(1, 0, 2).reshape(3, C)
              for b in (L0_conv_b_qkv, no_bias)]
    norms = [(L0_conv_gamma, L0_conv_beta), (L1_conv_gn_w, L1_conv_gn_b)]
    arrays = {
        "x_dram": np.ascontiguousarray(np.asarray(x).reshape(B, CT, P, S)),
        "w_qkv_dram": np.stack([qkv(np.asarray(w)) for w in (L0_conv_w_qkv, L1_conv_qkv_w)]),
        "w_proj_dram": np.stack([tiles(np.asarray(w).T) for w in (L0_conv_w_proj, L1_conv_proj_w)]),
        "pars_dram": np.stack([np.concatenate([columns(np.asarray(a)) for a in (g, b, bias[0], bias[1])], axis=1)
                               for (g, b), bias in zip(norms, biases)]),
        "bias_v_dram": np.stack([np.ascontiguousarray(np.broadcast_to(np.tile(bias[2], HALF // C), (P, HALF)))
                                 for bias in biases]),
        "bias_proj_dram": np.stack([np.ascontiguousarray(columns(np.asarray(b)))
                                    for b in (L0_conv_b_proj, L1_conv_proj_b)]),
        "ident_dram": np.eye(P, dtype=np.float32),
        "group_dram": np.kron(np.eye(P * GROUPS // C), np.full((C // GROUPS,) * 2, GROUPS / C / QUARTERS)).astype(np.float32),
    }
    nc = bacc.Bacc("TRN2", target_bir_lowering=False, num_devices=1)
    args = [nc.dram_tensor(name, a.shape, F32, kind="ExternalInput").ap() for name, a in arrays.items()]
    out = nc.dram_tensor("out_dram", [B, CT, P, S], F32, kind="ExternalOutput").ap()
    attention_layers(nc, *args, out)
    r = run_bass_kernel_spmd(nc, [arrays], core_ids=[0])
    return r.results[0]["out_dram"].reshape(_OUT)
```

```python
from contextlib import ExitStack

import numpy as np

import concourse.bass as bass
from concourse import mybir

F32 = mybir.dt.float32
F32R = mybir.dt.float32r
ALU = mybir.AluOpType
ACT = mybir.ActivationFunctionType
AX = mybir.AxisListType

LAYERS, B, C, S = 2, 8, 256, 1024
HEADS, GROUPS = 8, 32
EPS = 1e-5
HD = C // HEADS
SCALE = float(HD) ** -0.5
P = 128
CT = C // P
HG = HEADS // CT
NT = S // P
HALF = 512
NH = S // HALF
BLOCKS = LAYERS * B
SLOTS = BLOCKS * CT
UNITS = NH * NT * HG
KROWS = 3 * HD
MROW = KROWS
POOLED = 7
ADDS = POOLED - 1
POOLED_LAST = 4
QUARTERS = 2 * NH
STAGE_DMAS = 2 * 3
MAX_BANKS = 3
MAX_GROUP = HG * NH
LEAD = 4
AHEAD = NT * HG + LEAD
LATER = 1
PV_AT = 3
DENSE_AT = 1
SUMS_AT = 10
ROW_AT = 7
DIVIDE_AT = (1, 2, 2, 3)
BREAK_AT = 36
STATS_AT = (23, 26, 28, 33)
GN_AT = 51
NORMALISE_AT = (13, 17, 25, 29)
LOOP_FROM, LOOP_SLOTS = 1, 4
LOOPS = (SLOTS - 4) // LOOP_SLOTS


class Slot:

    def __init__(self, n, j, phase):
        self.n, self.j = n, j
        self.g = phase % 2
        self.qk = phase % 2
        self.v = (phase // 2) % 2
        self.phase = phase


def plain(n):
    return Slot(n, n // 2, n % 4)


def looped(i, k):
    return Slot(LOOP_SLOTS * i + LOOP_FROM + k, 2 * i + (LOOP_FROM + k) // 2, (LOOP_FROM + k) % 4)


def run_slots(eng, slot):
    slot(plain(0), first=True)
    with eng.Fori(0, LOOPS) as i:
        for k in range(LOOP_SLOTS):
            slot(looped(i, k))
    for n in range(LOOP_FROM + LOOPS * LOOP_SLOTS, SLOTS):
        slot(plain(n), has_next=n + 1 < SLOTS, has_second=n + 2 < SLOTS, has_third=n + 3 < SLOTS)


def max_unit_at(n, u):
    w = AHEAD + u
    return (n, w) if w < UNITS else (n + 1, w - UNITS)


def max_row_at(n, u):
    e = (AHEAD + u - ROW_AT) // MAX_GROUP
    return (n, e) if e < NT else (n + 1, e - NT)


def max_bank(u):
    if u < BREAK_AT:
        return u % MAX_BANKS
    return 1 if u == BREAK_AT else (u - 1) % MAX_BANKS


def attention_layers(nc, x, w_qkv, w_proj, pars, bias_v, bias_proj, ident_in, group_in, out):
    nc.disable_value_cache = True
    ctx = ExitStack()
    with ctx:
        def sb(name, shape, dt=F32):
            return ctx.enter_context(nc.sbuf_tensor(name, shape, dt))

        def bank(name):
            return ctx.enter_context(nc.psum_tensor(name, [P, HALF], F32))

        def sem(name):
            return ctx.enter_context(nc.semaphore(name))

        between = nc.dram_tensor("between", [B, CT, P, S], F32).ap()

        wq = sb("wq", [P, CT, 3 * C])
        wp = sb("wp", [P, CT, C])
        bv = sb("bv", [P, HALF])
        par = sb("par", [P, 2, 8])
        bp = sb("bp", [P, CT])
        ident = sb("ident", [P, P])
        group = sb("group", [P, P])
        ones = sb("ones", [P, HD])
        eps = sb("eps", [P, CT])
        neg_half = sb("neg_half", [P, CT])
        xn = [sb(f"xn{b}", [P, CT, S]) for b in range(2)]
        stats = sb("stats", [P, CT, NH, 6])
        mv = sb("mv", [P, CT, QUARTERS, 2])
        sq4 = sb("sq4", [P, CT, QUARTERS])
        channel_mv = sb("channel_mv", [P, CT, 2])
        inv_count = sb("inv_count", [P, CT, QUARTERS])
        sq = sb("sq", [P, CT])
        gm = sb("gm", [P, CT, 2])
        var = sb("var", [P, CT])
        rstd = sb("rstd", [P, CT])
        gn_a = sb("gn_a", [P, CT])
        gn_c = sb("gn_c", [P, CT])
        stage = {w: sb("stage_" + w, [P, S], F32R) for w in ("qh", "ql", "kh", "kl")}
        qs = [sb(f"qs{b}", [P, HG, S], F32R) for b in range(2)]
        ks = [sb(f"ks{b}", [P, HG, S], F32R) for b in range(2)]
        v = [sb(f"v{b}", [P, NT, C]) for b in range(2)]
        pt = [sb(f"pt{b}", [P, HG, HALF]) for b in range(4)]
        acc = [sb(f"acc{b}", [P, HG, HALF]) for b in range(NH)]
        raw_max = sb("raw_max", [P, 2, NT // NH, NH])
        neg_max = sb("neg_max", [P, 2, NT // NH])
        raw = sb("raw", [P, HALF])
        turned = sb("turned", [P, HALF])
        rden = sb("rden", [P, HALF // HD])
        att = sb("att", [P, CT, S])
        res = sb("res", [P, CT * NH, HALF])

        ps_t = [bank(f"ps_t{b}") for b in range(2)]
        ps_m = [bank(f"ps_m{b}") for b in range(MAX_BANKS)]
        ps_v = bank("ps_v")
        ps_d = bank("ps_d")
        ps_a = bank("ps_a")

        loaded = sem("constants_loaded")
        weights = sem("weights_loaded")
        wproj_loaded = sem("wproj_loaded")
        x_loaded = sem("x_loaded")
        res_loaded = sem("res_loaded")
        stored = sem("stored")
        staged = [sem(f"staged_head{h}") for h in range(HG)]
        constants_set = sem("constants_set")
        ones_row_set = sem("ones_row_set")
        bn_done = sem("bn_done")
        mv_done = sem("mv_done")
        mv_summed = sem("mv_summed")
        gm_ready = sem("gm_ready")
        gm_done = sem("gm_done")
        gn_step = sem("gn_step")
        xn_done = sem("xn_done")
        qk_ready = sem("qk_ready")
        qkh_done = sem("qkh_done")
        qkl_done = sem("qkl_done")
        v_ready = sem("v_ready")
        v_done = sem("v_done")
        proj_ready = sem("proj_ready")
        proj_done = sem("proj_done")
        sm_ready = sem("sm_ready")
        max_done = sem("max_done")
        neg_done = sem("neg_done")
        mrow_ready = sem("mrow_ready")
        mrow_done = sem("mrow_done")
        st_ready = sem("st_ready")
        exp_done = sem("exp_done")
        pv_done = sem("pv_done")
        pool_added = sem("pool_added")
        sum_ready = sem("sum_ready")
        raw_done = sem("raw_done")
        divide_step = sem("divide_step")
        norm_done = sem("norm_done")

        start_banks = [ps_d] + ps_m

        block = ctx.enter_context(nc.Block())

        @block.sync
        def _(sp):
            def load_block(layer, src, image, parity):
                for ct in range(CT):
                    sp.dma_start(xn[parity][:, ct, :], src[image, ct]).then_inc(x_loaded, 16)
                sp.dma_start(par[:, parity, :], pars[layer]).then_inc(x_loaded, 16)

            def load_weights(layer):
                sp.dma_start(wq[:, :, :], w_qkv[layer]).then_inc(weights, 16)
                sp.dma_start(bv[:, :], bias_v[layer]).then_inc(weights, 16)

            def load_residual(layer, src, image):
                for ct in range(CT):
                    sp.dma_start(res[:, NH * ct:NH * ct + NH, :],
                                 src[image, ct].rearrange("p (h s) -> p h s", h=NH)).then_inc(res_loaded, 16)
                sp.dma_start(bp[:, :], bias_proj[layer]).then_inc(res_loaded, 16)

            def store_block(dst, j, image):
                for piece in range(CT * NH):
                    sp.wait_ge(proj_done, CT * NH * j + piece + 1)
                    h, ct = piece // CT, piece % CT
                    sp.dma_start(dst[image, ct][:, h * HALF:(h + 1) * HALF],
                                 res[:, NH * ct + h, :]).then_inc(stored, 16)

            def stage_slot(n, b):
                sp.wait_ge(qkl_done, 4 * n + 4)
                for h in range(HG):
                    for dst, parts in ((ks[b], ("kh", "kl", "kh")), (qs[b], ("qh", "qh", "ql"))):
                        for r, part in enumerate(parts):
                            sp.dma_start(dst[HD * r:HD * (r + 1), h, :].bitcast(F32),
                                         stage[part][HD * h:HD * (h + 1), :].bitcast(F32)).then_inc(staged[h], 16)

            load_block(0, x, 0, 0)
            sp.dma_start(group[:, :], group_in).then_inc(loaded, 16)
            sp.dma_start(ident[:, :], ident_in).then_inc(loaded, 16)
            load_weights(0)
            sp.wait_ge(x_loaded, 48)
            load_block(0, x, 1, 1)
            sp.dma_start(wp[:, :, :], w_proj[0]).then_inc(wproj_loaded, 16)
            stage_slot(0, 0)
            stage_slot(1, 1)

            def body(i, next_layer, done_layer):
                nsrc = x if next_layer == 0 else between
                dsrc, ddst = (x, between) if done_layer == 0 else (between, out)
                for k in range(LOOP_SLOTS):
                    s = looped(i, k)
                    if isinstance(i, int) and s.n == 2 * B - 2:
                        sp.wait_ge(qk_ready, 4 * 2 * B)
                        sp.wait_ge(v_done, 4 * B)
                        load_weights(1)
                        sp.wait_ge(weights, 64)
                    if s.g == 1:
                        sp.wait_ge(qkl_done, 4 * (2 * s.j + 2))
                        load_block(next_layer, nsrc, s.j + 2 - B * next_layer, s.v)
                    sp.wait_ge(st_ready, UNITS * s.n)
                    stage_slot(s.n + 1, 1 - s.qk)
                    if s.g == 1:
                        if not (isinstance(s.j, int) and s.j == 0):
                            sp.wait_ge(stored, 16 * CT * NH * s.j)
                        load_residual(done_layer, dsrc, s.j - B * done_layer)
                        continue
                    store_block(ddst, s.j - 1, s.j - 1 - B * done_layer)
                    if isinstance(i, int) and s.j == B:
                        sp.dma_start(wp[:, :, :], w_proj[1]).then_inc(wproj_loaded, 16)
                        sp.wait_ge(wproj_loaded, 32)

            turn = B // 2 - 1
            body(0, 0, 0)
            with sp.Fori(1, turn) as i:
                body(i, 0, 0)
            body(turn, 1, 0)
            with sp.Fori(turn + 1, LOOPS) as i:
                body(i, 1, 1)
            for n in range(LOOP_FROM + LOOPS * LOOP_SLOTS, SLOTS):
                s = plain(n)
                if n + 1 < SLOTS:
                    sp.wait_ge(st_ready, UNITS * n)
                    stage_slot(n + 1, 1 - s.qk)
                if s.g == 1:
                    sp.wait_ge(stored, 16 * CT * NH * s.j)
                    load_residual(1, between, s.j - B)
                else:
                    store_block(out, s.j - 1, s.j - 1 - B)
            store_block(out, BLOCKS - 1, B - 1)
            sp.wait_ge(stored, 16 * CT * NH * BLOCKS)

        @block.tensor
        def _(pe):
            def aux_free(mrows, sums, stats_done=None):
                if not (isinstance(mrows, int) and mrows == 0):
                    pe.wait_ge(mrow_done, mrows)
                if not (isinstance(sums, int) and sums == 0):
                    pe.wait_ge(norm_done, sums)
                if stats_done is not None:
                    pe.wait_ge(gm_done, stats_done)

            def scores_t(s, u):
                hf, t, h = u // (NT * HG), u // HG % NT, u % HG
                if not (isinstance(s.n, int) and UNITS * s.n + u < 2):
                    pe.wait_ge(exp_done, UNITS * s.n + u - 1)
                if t == 0:
                    pe.wait_ge(mrow_done, NT * s.n + HG * hf + h + 1)
                pe.matmul(ps_t[u % 2][:, :], ks[s.qk][0:KROWS + 1, h, t * P:(t + 1) * P],
                          qs[s.qk][0:KROWS + 1, h, hf * HALF:(hf + 1) * HALF],
                          start=True, stop=True).then_inc(st_ready, 1)

            def scores_for_max(slot_n, slot_qk, u):
                n, w = max_unit_at(slot_n, u)
                b = slot_qk if w >= AHEAD else 1 - slot_qk
                hf, h, t, kf = w // (NT * HG), w // MAX_GROUP % HG, w // NH % (NT // NH), w % NH
                if w % MAX_GROUP == 0 and hf == 0:
                    pe.wait_ge(staged[h], 16 * STAGE_DMAS * (n + 1))
                back = next(k for k in range(1, UNITS) if max_bank((u - k) % UNITS) == max_bank(u))
                if not isinstance(n, int) or UNITS * n + w >= back:
                    pe.wait_ge(max_done, UNITS * n + w - back + 1)
                c = hf * HALF + t * P
                pe.matmul(ps_m[max_bank(u)][:, :], qs[b][0:KROWS, h, c:c + P],
                          ks[b][0:KROWS, h, kf * HALF:(kf + 1) * HALF],
                          start=True, stop=True).then_inc(sm_ready, 1)

            def max_rows(n, e, sums, stats_done=None):
                pe.wait_ge(neg_done, NT * n + e + 1)
                aux_free(NT * n + e, sums, stats_done)
                for t in range(NT // NH):
                    mm = pe.matmul(ps_a[MROW:MROW + 1, t * P:(t + 1) * P], neg_max[:, e % 2, t:t + 1],
                                   ident[:, :], start=True, stop=True)
                mm.then_inc(mrow_ready, 1)

            def weighted_values(s, hf, t):
                half = NH * s.n + hf
                pe.wait_ge(exp_done, HG * (NT * half + t + 1))
                if t == 0:
                    if not (isinstance(half, int) and half == 0):
                        pe.wait_ge(raw_done, half)
                    if hf == 0:
                        pe.wait_ge(v_done, 4 * s.j + 4)
                for h in range(HG):
                    c = (s.g * HG + h) * HD
                    mm = pe.matmul(ps_v[HD * h:HD * (h + 1), :], v[s.v][:, t, c:c + HD],
                                   pt[t % 4][:, h, :], start=(t == 0), stop=(t == NT - 1))
                mm.then_inc(pv_done, 1)

            def sums(s, hf, mrows, pooled=POOLED):
                half = NH * s.n + hf
                pe.wait_ge(pool_added, ADDS * half + pooled - 1)
                aux_free(mrows, half)
                tiles = [pt[t % 4] for t in range(pooled, NT)] + [acc[hf]]
                for k, tile in enumerate(tiles):
                    for h in range(HG):
                        mm = pe.matmul(ps_a[HD * h:HD * (h + 1), :], ones[:, :], tile[:, h, :],
                                       start=(k == 0), stop=(k == len(tiles) - 1))
                mm.then_inc(sum_ready, 1)

            def project_qk(g, parity, r, kt, bank=ps_d):
                which, hf = r // NH, r % NH
                c = which * C + g * P
                mm = pe.matmul(bank[:, :], wq[:, kt, c:c + P], xn[parity][:, kt, hf * HALF:(hf + 1) * HALF],
                               start=(kt == 0), stop=(kt == CT - 1))
                if kt == CT - 1:
                    mm.then_inc(qk_ready, 1)

            def project_v(parity, r, t, bank=ps_d):
                for kt in range(CT):
                    mm = pe.matmul(bank[:, t * C:(t + 1) * C], xn[parity][:, kt, (2 * r + t) * P:(2 * r + t + 1) * P],
                                   wq[:, kt, 2 * C:3 * C], start=(kt == 0), stop=(kt == CT - 1))
                if t == 1:
                    mm.then_inc(v_ready, 1)

            def project_out(piece, kt):
                hf, ct = piece // CT, piece % CT
                mm = pe.matmul(ps_d[:, :], wp[:, kt, ct * P:(ct + 1) * P],
                               att[:, kt, hf * HALF:(hf + 1) * HALF], start=(kt == 0), stop=(kt == CT - 1))
                if kt == CT - 1:
                    mm.then_inc(proj_ready, 1)

            def group_stats(j, mrows, nsums):
                pe.wait_ge(mv_summed, j + 1)
                aux_free(mrows, nsums)
                mm = pe.matmul(ps_a[:, 0:2 * CT], group[:, :], channel_mv[:, :, :], start=True, stop=True)
                mm.then_inc(gm_ready, 1)

            def dense(s, u, first, has_next, has_second):
                step = u // HG
                r, part = step // 2 % 4, step % 2
                if step < UNITS // HG // 2:
                    if s.g == 0 and not first:
                        if part == 0:
                            if r == 0:
                                pe.wait_ge(qkl_done, 4 * (s.n + 1) + 4)
                            else:
                                pe.wait_ge(proj_done, 4 * (s.j - 1) + r)
                            pe.wait_ge(norm_done, NH * s.n - 1 + r // CT)
                        project_out(r, part)
                    if s.g == 1 and has_second:
                        if part == 0:
                            if r == 0:
                                pe.wait_ge(qkl_done, 4 * (s.n + 1) + 4)
                            else:
                                pe.wait_ge(v_done, 4 * (s.j + 1) + r)
                        project_v(1 - s.v, r, part)
                elif has_second:
                    if part == 0:
                        if r:
                            pe.wait_ge(qkl_done, 4 * (s.n + 2) + r)
                        elif s.g == 1:
                            pe.wait_ge(v_done, 4 * (s.j + 1) + 4)
                        else:
                            pe.wait_ge(xn_done, CT * NH * (s.j + 2))
                            if not first:
                                pe.wait_ge(proj_done, 4 * s.j)
                    project_qk(s.g, 1 - s.v, r, part)
                elif not has_next and step >= LAST_OUT:
                    piece, part = (step - LAST_OUT) // 2, (step - LAST_OUT) % 2
                    if part == 0:
                        pe.wait_ge(proj_done, 4 * s.j + piece)
                        pe.wait_ge(norm_done, NH * s.n + 1)
                    project_out(piece, part)

            def slot(s, first=False, has_next=True, has_second=True, has_third=True):
                prev = None if first else Slot(s.n - 1, s.j - (1 - s.g), (s.phase + 3) % 4)
                sums_before = NH * s.n - (not first)
                rows_before = NT * s.n + HG
                stats_done = None
                for u in range(UNITS):
                    scores_t(s, u)
                    if u % HG == DENSE_AT:
                        dense(s, u, first, has_next, has_second)
                    if has_next or AHEAD + u < UNITS:
                        scores_for_max(s.n, s.qk, u)
                    if u == SUMS_AT and not first:
                        sums(prev, NH - 1, rows_before)
                        sums_before = sums_before + 1
                    if u == SUMS_AT + UNITS // NH:
                        sums(s, 0, rows_before)
                        sums_before = sums_before + 1
                    if u % HG == PV_AT:
                        done = u // HG - 1
                        if done >= 0:
                            weighted_values(s, done // NT, done % NT)
                        elif not first:
                            weighted_values(prev, NH - 1, NT - 1)
                    if u % MAX_GROUP == ROW_AT and (has_next or max_row_at(0, u)[0] == 0):
                        max_rows(*max_row_at(s.n, u), sums_before, stats_done)
                        rows_before, stats_done = rows_before + 1, None
                    if s.g == 1 and has_third and u == GN_AT:
                        group_stats(s.j + 2, rows_before, sums_before)
                        stats_done = s.j + 3

            pe.wait_ge(loaded, 32)
            group_stats(0, 0, 0)
            pe.wait_ge(weights, 32)
            pe.wait_ge(wproj_loaded, 16)
            pe.wait_ge(xn_done, CT * NH)
            for r in range(4):
                for kt in range(CT):
                    project_qk(0, 0, r, kt, start_banks[r])
            for r in range(4):
                pe.wait_ge(qkl_done, r + 1)
                for t in range(2):
                    project_v(0, r, t, start_banks[r])
            group_stats(1, 0, 0)
            pe.wait_ge(v_done, 4)
            pe.wait_ge(ones_row_set, 2)
            for w in range(AHEAD):
                scores_for_max(-1, 1, w - AHEAD + UNITS)
                if w % MAX_GROUP == 0 and w // MAX_GROUP < 4:
                    r = w // MAX_GROUP
                    if r:
                        pe.wait_ge(qkl_done, 4 + r)
                    for kt in range(CT):
                        project_qk(1, 0, r, kt)
                if w % MAX_GROUP == 3 and w > MAX_GROUP:
                    max_rows(0, w // MAX_GROUP - 1, 0, 2)
            run_slots(pe, slot)
            last = plain(SLOTS - 1)
            weighted_values(last, NH - 1, NT - 1)
            sums(last, NH - 1, NT * SLOTS, POOLED_LAST)
            for piece in range(CT, CT * NH):
                pe.wait_ge(proj_done, 4 * (BLOCKS - 1) + piece)
                if piece == CT:
                    pe.wait_ge(norm_done, NH * SLOTS)
                for kt in range(CT):
                    project_out(piece, kt)

        @block.scalar
        def _(act):
            def exp(s, u):
                half_of, t, h = u // (NT * HG), u // HG % NT, u % HG
                half = NH * s.n + half_of
                started = not (isinstance(half, int) and half == 0 and t < 4)
                if h == 0 and started:
                    act.wait_ge(pv_done, NT * half + t - 3)
                    if t >= 4:
                        act.wait_ge(pool_added, ADDS * half + max(1, t - 4))
                    elif t + 4 < POOLED:
                        act.wait_ge(pool_added, ADDS * (half - 1) + t + 4)
                    else:
                        act.wait_ge(sum_ready, half)
                act.wait_ge(st_ready, UNITS * s.n + u + 1)
                act.activation(pt[t % 4][:, h, :], ps_t[u % 2][:, :], ACT.Exp, scale=SCALE).then_inc(exp_done, 1)

            def max_row(n, b, e):
                hf, h = e // HG, e % HG
                act.wait_ge(mrow_ready, NT * n + e + 1)
                act.activation(qs[b][MROW:MROW + 1, h, hf * HALF:(hf + 1) * HALF], ps_a[MROW:MROW + 1, :],
                               ACT.Identity).then_inc(mrow_done, 1)

            def values_out(half):
                act.wait_ge(pv_done, NT * half + NT)
                if not (isinstance(half, int) and half == 0):
                    act.wait_ge(norm_done, half)
                act.activation(raw[:, :], ps_v[:, :], ACT.Identity).then_inc(raw_done, 1)

            def qk_high(n, g, parity, r, bank=ps_d):
                which, hf = r // NH, r % NH
                if r == 0 and not (isinstance(n, int) and n == 0):
                    for h in range(HG):
                        act.wait_ge(staged[h], 16 * STAGE_DMAS * n)
                act.wait_ge(qk_ready, 4 * n + r + 1)
                dst = stage["qh" if which == 0 else "kh"]
                act.activation(dst[:, hf * HALF:(hf + 1) * HALF], bank[:, :], ACT.Identity,
                               bias=par[:, parity, 4 + 2 * which + g:5 + 2 * which + g]).then_inc(qkh_done, 1)

            def group_stats_out(j):
                act.wait_ge(gm_ready, j + 1)
                act.activation(gm[:, :, :], ps_a[:, 0:2 * CT].rearrange("p (c k) -> p c k", c=CT),
                               ACT.Identity).then_inc(gm_done, 1)

            def normalise(j, parity, part):
                ct, cols = part // NH, slice(part % NH * HALF, (part % NH + 1) * HALF)
                act.wait_ge(gn_step, GN_STEPS * (j + 1))
                act.activation(xn[parity][:, ct, cols], xn[parity][:, ct, cols], ACT.Identity,
                               scale=gn_a[:, ct:ct + 1], bias=gn_c[:, ct:ct + 1]).then_inc(xn_done, 1)

            def slot(s, first=False, has_next=True, has_second=True, has_third=True):
                for u in range(UNITS):
                    exp(s, u)
                    if u == PV_AT + LATER and not first:
                        values_out(NH * s.n - 1)
                    if u == PV_AT + LATER + UNITS // NH:
                        values_out(NH * s.n)
                    if u % MAX_GROUP == ROW_AT and (has_next or max_row_at(0, u)[0] == 0):
                        n, e = max_row_at(s.n, u)
                        max_row(n, s.qk if e >= HG else 1 - s.qk, e)
                    if s.g == 1 and has_third and u == GN_AT + LATER:
                        group_stats_out(s.j + 2)
                    if s.g == 0 and has_second and not first and u in NORMALISE_AT:
                        normalise(s.j + 1, 1 - s.v, NORMALISE_AT.index(u))
                    if has_second and u >= UNITS // 2 and u % (2 * HG) == DENSE_AT + HG + LATER:
                        qk_high(s.n + 2, s.g, 1 - s.v, (u - UNITS // 2) // (2 * HG))

            group_stats_out(0)
            for part in range(CT * NH):
                normalise(0, 0, part)
            for r in range(4):
                qk_high(0, 0, 0, r, start_banks[r])
            group_stats_out(1)
            for part in range(CT * NH):
                normalise(1, 1, part)
            for r in range(4):
                qk_high(1, 1, 0, r)
                if r:
                    max_row(0, 0, r - 1)
            max_row(0, 0, HG - 1)
            run_slots(act, slot)
            values_out(NH * SLOTS - 1)

        @block.vector
        def _(dve):
            def max_unit(slot_n, u):
                n, w = max_unit_at(slot_n, u)
                e, t, kf = w // MAX_GROUP, w // NH % (NT // NH), w % NH
                dve.wait_ge(sm_ready, UNITS * n + w + 1)
                if w % MAX_GROUP == 0 and not (isinstance(n, int) and NT * n + e < 2):
                    dve.wait_ge(neg_done, NT * n + e - 1)
                dve.tensor_reduce(raw_max[:, e % 2, t, kf:kf + 1], ps_m[max_bank(u)][:, :], AX.X, ALU.max)\
                   .then_inc(max_done, 1)
                if w % MAX_GROUP == MAX_GROUP - 1:
                    dve.wait_ge(max_done, UNITS * n + w + 1)
                    if not (isinstance(n, int) and NT * n + e < 2):
                        dve.wait_ge(mrow_ready, NT * n + e - 1)
                    dve.tensor_reduce(neg_max[:, e % 2, :], raw_max[:, e % 2, :, :], AX.X, ALU.max,
                                      negate=True).then_inc(neg_done, 1)

            def qk_low(n, g, parity, r, bank=ps_d):
                which, hf = r // NH, r % NH
                cols = slice(hf * HALF, (hf + 1) * HALF)
                hi, lo = (stage["qh"], stage["ql"]) if which == 0 else (stage["kh"], stage["kl"])
                dve.wait_ge(qkh_done, 4 * n + r + 1)
                dve.scalar_tensor_tensor(out=lo[:, cols], in0=bank[:, :],
                                         scalar=par[:, parity, 4 + 2 * which + g:5 + 2 * which + g],
                                         in1=hi[:, cols].bitcast(F32), op0=ALU.add,
                                         op1=ALU.subtract).then_inc(qkl_done, 1)

            def v_out(j, parity, r, bank=ps_d):
                dve.wait_ge(v_ready, 4 * j + r + 1)
                dve.tensor_tensor(v[parity][:, 2 * r:2 * r + 2, :], bank[:, :].rearrange("p (t c) -> p t c", t=2),
                                  bv[:, :].rearrange("p (t c) -> p t c", t=2), ALU.add).then_inc(v_done, 1)

            def channel_stats(j, parity, part):
                ct, hf = part // NH, part % NH
                if part == 0:
                    dve.wait_ge(x_loaded, 48 * (j + 1))
                dve.bn_stats(stats[:, ct, hf, :], xn[parity][:, ct, hf * HALF:(hf + 1) * HALF]).then_inc(bn_done, 1)

            def add_quarters(j):
                dve.wait_ge(mv_done, MV_STEPS * (j + 1))
                dve.tensor_reduce(channel_mv[:, :, :], mv[:, :, :, :].rearrange("p c q k -> p c k q"),
                                  AX.X, ALU.add).then_inc(mv_summed, 1)

            def divide(half, g, hf, step):
                if step == 0:
                    dve.wait_ge(sum_ready, half + 1)
                    dve.transpose(turned[:, :], ps_a[:, :]).then_inc(divide_step, 1)
                elif step == 1:
                    dve.wait_ge(divide_step, 3 * half + 1)
                    dve.reciprocal(rden[:, :], turned[:, 0:HALF:HD]).then_inc(divide_step, 1)
                elif step == 2:
                    dve.wait_ge(divide_step, 3 * half + 2)
                    dve.transpose(ps_a[:, :], rden[:, :].unsqueeze(2).to_broadcast([P, HALF // HD, HD]))\
                       .then_inc(divide_step, 1)
                else:
                    dve.wait_ge(raw_done, half + 1)
                    dve.wait_ge(divide_step, 3 * half + 3)
                    dve.tensor_tensor(att[:, g, hf * HALF:(hf + 1) * HALF], raw[:, :], ps_a[:, :],
                                      ALU.mult).then_inc(norm_done, 1)

            def project_out(j, piece):
                hf, ct = piece // CT, piece % CT
                if piece == 0:
                    dve.wait_ge(res_loaded, 48 * (j + 1))
                dve.wait_ge(proj_ready, 4 * j + piece + 1)
                r = res[:, NH * ct + hf, :]
                dve.scalar_tensor_tensor(out=r, in0=ps_d[:, :], scalar=bp[:, ct:ct + 1], in1=r,
                                         op0=ALU.add, op1=ALU.add).then_inc(proj_done, 1)

            def slot(s, first=False, has_next=True, has_second=True, has_third=True):
                for u in range(UNITS):
                    if u % (2 * HG) == DENSE_AT + HG + LATER:
                        r = u // (2 * HG) % 4
                        if u < UNITS // 2 and s.g == 0 and not first:
                            project_out(s.j - 1, r)
                        if u < UNITS // 2 and s.g == 1 and has_second:
                            v_out(s.j + 1, 1 - s.v, r)
                        if not has_next and (u - LATER) // HG > LAST_OUT:
                            project_out(s.j, ((u - LATER) // HG - LAST_OUT) // 2)
                    if has_second and u >= UNITS // 2 and u % (2 * HG) == DENSE_AT + HG + 2 * LATER:
                        qk_low(s.n + 2, s.g, 1 - s.v, (u - UNITS // 2) // (2 * HG))
                    if has_next or AHEAD + u < UNITS:
                        max_unit(s.n, u)
                    for step, at in enumerate(DIVIDE_AT):
                        if u == SUMS_AT + at and not first:
                            divide(NH * s.n - 1, 1 - s.g, NH - 1, step)
                        if u == SUMS_AT + UNITS // NH + at:
                            if s.g == 0 and not first and step == len(DIVIDE_AT) - 1:
                                dve.wait_ge(proj_ready, 4 * s.j)
                            divide(NH * s.n, s.g, 0, step)
                    if s.g == 1 and has_third and u in STATS_AT:
                        channel_stats(s.j + 2, s.v, STATS_AT.index(u))
                    if s.g == 1 and has_third and u == GN_AT - 1:
                        add_quarters(s.j + 2)

            for part in range(CT * NH):
                channel_stats(0, 0, part)
            add_quarters(0)
            for r in range(4):
                qk_low(0, 0, 0, r, start_banks[r])
            dve.wait_ge(weights, 32)
            for r in range(4):
                v_out(0, 0, r, start_banks[r])
            for part in range(CT * NH):
                channel_stats(1, 1, part)
            add_quarters(1)
            for w in range(AHEAD):
                max_unit(-1, w - AHEAD + UNITS)
                if w % MAX_GROUP == 2 and w // MAX_GROUP < 4:
                    qk_low(1, 1, 0, w // MAX_GROUP)
            run_slots(dve, slot)
            for step in range(len(DIVIDE_AT)):
                divide(NH * SLOTS - 1, 1, NH - 1, step)
            for piece in range(CT, CT * NH):
                project_out(BLOCKS - 1, piece)

        @block.gpsimd
        def _(pool):
            def mean_square(j):
                pool.wait_ge(bn_done, CT * NH * (j + 1))
                parts = stats[:, :, :, :].rearrange("p c h (o k) -> p c (h o) k", o=2)
                mean, m2 = parts[:, :, :, 1], parts[:, :, :, 2]
                pool.tensor_tensor(sq4[:, :, :], mean, mean, ALU.mult).then_inc(mv_done, 1)
                pool.tensor_tensor(mv[:, :, :, 1], m2, inv_count[:, :, :], ALU.mult).then_inc(mv_done, 1)
                pool.tensor_copy(mv[:, :, :, 0], mean).then_inc(mv_done, 1)
                pool.wait_ge(mv_done, MV_STEPS * j + 3)
                pool.tensor_tensor(mv[:, :, :, 1], mv[:, :, :, 1], sq4[:, :, :], ALU.add).then_inc(mv_done, 1)

            def scale_and_shift(j, parity):
                pool.wait_ge(gm_done, j + 1)
                step = [0]

                def then(ins):
                    ins.then_inc(gn_step, 1)
                    step[0] += 1
                    pool.wait_ge(gn_step, GN_STEPS * j + step[0])

                then(pool.tensor_tensor(sq[:, :], gm[:, :, 0], gm[:, :, 0], ALU.mult))
                then(pool.tensor_tensor(var[:, :], gm[:, :, 1], sq[:, :], ALU.subtract))
                then(pool.tensor_tensor(var[:, :], var[:, :], eps[:, :], ALU.add))
                then(pool.tensor_tensor(rstd[:, :], var[:, :], neg_half[:, :], ALU.pow))
                then(pool.tensor_tensor(gn_a[:, :], rstd[:, :], par[:, parity, 0:2], ALU.mult))
                then(pool.tensor_tensor(sq[:, :], gm[:, :, 0], gn_a[:, :], ALU.mult))
                then(pool.tensor_tensor(gn_c[:, :], par[:, parity, 2:4], sq[:, :], ALU.subtract))

            def add(half, hf, t):
                pool.wait_ge(exp_done, HG * (NT * half + t + 1))
                if t == 1:
                    if not (isinstance(half, int) and half < NH):
                        pool.wait_ge(sum_ready, half - 1)
                    a = pt[0]
                else:
                    pool.wait_ge(pool_added, ADDS * half + t - 1)
                    a = acc[hf]
                pool.tensor_tensor(acc[hf][:, :, :], a[:, :, :], pt[t % 4][:, :, :], ALU.add).then_inc(pool_added, 1)

            def slot(s, first=False, has_next=True, has_second=True, has_third=True):
                for hf in range(NH):
                    for t in range(1, POOLED if has_next or hf < NH - 1 else POOLED_LAST):
                        add(NH * s.n + hf, hf, t)
                        if s.g == 1 and has_third and hf == 1 and t == 1:
                            mean_square(s.j + 2)
                        if s.g == 1 and has_third and hf == 1 and t == 4:
                            scale_and_shift(s.j + 2, s.v)

            for tile, value in ((ones, 1.0), (neg_half, -0.5), (eps, EPS)):
                pool.memset(tile[:, :], value).then_inc(constants_set, 1)
            pool.memset(inv_count[:, :, :], QUARTERS / S).then_inc(constants_set, 1)
            pool.wait_ge(constants_set, 4)
            mean_square(0)
            scale_and_shift(0, 0)
            for b in range(2):
                pool.memset(ks[b][MROW:MROW + 1, :, :].bitcast(F32), 1.0).then_inc(ones_row_set, 1)
                pool.wait_ge(ones_row_set, b + 1)
            mean_square(1)
            scale_and_shift(1, 1)
            run_slots(pool, slot)


MV_STEPS = 4
GN_STEPS = 7
LAST_OUT = 12

_OUT = (B, C, 32, 32)


def kernel(x, L0_conv_gamma, L0_conv_beta, L0_conv_w_qkv, L0_conv_b_qkv, L0_conv_w_proj, L0_conv_b_proj,
           L1_conv_gn_w, L1_conv_gn_b, L1_conv_qkv_w, L1_conv_proj_w, L1_conv_proj_b):
    import concourse.bacc as bacc
    from concourse.bass_utils import run_bass_kernel_spmd

    def tiles(a):
        return np.ascontiguousarray(a.reshape(CT, P, -1).transpose(1, 0, 2))

    def qkv(w):
        return tiles(w.reshape(HEADS, 3, HD, C).transpose(3, 1, 0, 2).reshape(C, 3 * C))

    def columns(a):
        return a.reshape(CT, P).T

    no_bias = np.zeros(3 * C, np.float32)
    biases = [np.asarray(b).reshape(HEADS, 3, HD).transpose(1, 0, 2).reshape(3, C)
              for b in (L0_conv_b_qkv, no_bias)]
    norms = [(L0_conv_gamma, L0_conv_beta), (L1_conv_gn_w, L1_conv_gn_b)]
    arrays = {
        "x_dram": np.ascontiguousarray(np.asarray(x).reshape(B, CT, P, S)),
        "w_qkv_dram": np.stack([qkv(np.asarray(w)) for w in (L0_conv_w_qkv, L1_conv_qkv_w)]),
        "w_proj_dram": np.stack([tiles(np.asarray(w).T) for w in (L0_conv_w_proj, L1_conv_proj_w)]),
        "pars_dram": np.stack([np.concatenate([columns(np.asarray(a)) for a in (g, b, bias[0], bias[1])], axis=1)
                               for (g, b), bias in zip(norms, biases)]),
        "bias_v_dram": np.stack([np.ascontiguousarray(np.broadcast_to(np.tile(bias[2], HALF // C), (P, HALF)))
                                 for bias in biases]),
        "bias_proj_dram": np.stack([np.ascontiguousarray(columns(np.asarray(b)))
                                    for b in (L0_conv_b_proj, L1_conv_proj_b)]),
        "ident_dram": np.eye(P, dtype=np.float32),
        "group_dram": np.kron(np.eye(P * GROUPS // C), np.full((C // GROUPS,) * 2, GROUPS / C / QUARTERS)).astype(np.float32),
    }
    nc = bacc.Bacc("TRN2", target_bir_lowering=False, num_devices=1)
    args = [nc.dram_tensor(name, a.shape, F32, kind="ExternalInput").ap() for name, a in arrays.items()]
    out = nc.dram_tensor("out_dram", [B, CT, P, S], F32, kind="ExternalOutput").ap()
    attention_layers(nc, *args, out)
    r = run_bass_kernel_spmd(nc, [arrays], core_ids=[0])
    return r.results[0]["out_dram"].reshape(_OUT)
```
